# Optimizing a Trainium2 kernel written in Bass

```python
import numpy as np
import jax
import jax.numpy as jnp

def _softmax(x, axis=-1):
    return jax.nn.softmax(x, axis=axis)

def _gelu(x):
    return jax.nn.gelu(x, approximate=True)

def _silu(x):
    return jax.nn.silu(x)

def _sigmoid(x):
    return jax.nn.sigmoid(x)

def _layernorm(x, axis=-1, eps=1e-05):
    m = jnp.mean(x, axis=axis, keepdims=True)
    v = jnp.var(x, axis=axis, keepdims=True)
    return (x - m) / jnp.sqrt(v + eps)

def _scatter_add(tgt, idx, src, axis=0):
    return tgt.at[idx].add(src)

def _segment_sum(src, seg, n):
    return jax.ops.segment_sum(src, seg, n)
kernel_name = 'mk_gnn_preln_d1_gnn_r8_158ef4'

def setup_inputs(seed: int=0):
    np.random.seed(seed)
    _w = jnp.asarray

    def _rec_inputs():
        import jax
        import jax.numpy as jnp
        _gk = jax.random.key(seed)
        x = -0.0002117 + 1 * jax.random.normal(jax.random.fold_in(_gk, 1), (12500, 256), jnp.float32)
        src = jax.random.randint(jax.random.fold_in(_gk, 2), (200000,), 0, 12500, jnp.int32)
        dst = jnp.minimum((12500 * jax.random.uniform(jax.random.fold_in(_gk, 3), (200000,)) ** 2.0).astype(jnp.int32), 99999)
        _o = jnp.argsort(dst, stable=True)
        src = src[_o]
        dst = dst[_o]
        edge_type_500 = jax.random.randint(jax.random.fold_in(_gk, 12), (200000,), 0, 500, jnp.int32)
        return (x, src, dst, edge_type_500)
    x, src, dst, edge_type_500 = _rec_inputs()

    def _L0_gnn_setup():
        import jax, jax.numpy as jnp
        import numpy as np
        G = (1.0, 1.0)

        def to_hypercomplex(x, n_blades):
            return x.reshape(*x.shape[:-1], n_blades, -1).swapaxes(-2, -1)

        def clifford_kernel_2d(w, g):
            g0, g1 = g
            k0 = jnp.concatenate([w[0], g0 * w[1], g1 * w[2], -g0 * g1 * w[3]], axis=1)
            k1 = jnp.concatenate([w[1], w[0], -g1 * w[3], g1 * w[2]], axis=1)
            k2 = jnp.concatenate([w[2], g0 * w[3], w[0], -g0 * w[1]], axis=1)
            k3 = jnp.concatenate([w[3], w[2], w[1], w[0]], axis=1)
            return jnp.concatenate([k0, k1, k2, k3], axis=0)

        def clifford_linear(x, w, b, g=G):
            N = x.shape[0]
            k = clifford_kernel_2d(w, g)
            xf = x.swapaxes(-2, -1).reshape(N, -1)
            out = xf @ k.T + b.reshape(-1)
            C_out = w.shape[1]
            return out.reshape(N, 4, C_out).swapaxes(-2, -1)
        key = jax.random.key(seed)
        ks = jax.random.split(key, 10)
        N, E, R, emb_dim = (12500, 75000, 500, 256)
        C = emb_dim // 4
        s = 0.05
        return {'h': jax.random.normal(ks[0], (N, emb_dim), jnp.float32), 'edge_index': jax.random.randint(ks[1], (2, E), 0, N, jnp.int64), 'edge_type': jax.random.randint(ks[2], (E,), 0, R, jnp.int64), 'relation_emb': jax.random.normal(ks[3], (R, emb_dim), jnp.float32), 'msg_w': jax.random.normal(ks[4], (4, C, C), jnp.float32) * s, 'msg_b': jax.random.normal(ks[5], (4, C), jnp.float32) * s, 'upd_w': jax.random.normal(ks[6], (4, C, C), jnp.float32) * s, 'upd_b': jax.random.normal(ks[7], (4, C), jnp.float32) * s, 'gate_w': jax.random.normal(ks[8], (1, emb_dim), jnp.float32) * s, 'gate_b': jax.random.normal(ks[9], (1,), jnp.float32) * s}
    _L0_gnn_all = _L0_gnn_setup()
    _L0_gnn_in = {k: v for k, v in _L0_gnn_all.items() if k in ('relation_emb', 'msg_w', 'msg_b', 'upd_w', 'upd_b', 'gate_w', 'gate_b')}
    del _L0_gnn_all
    return {'x': x, 'src': src, 'dst': dst, 'edge_type_500': edge_type_500, 'L0_gnn_relation_emb': _L0_gnn_in['relation_emb'], 'L0_gnn_msg_w': _L0_gnn_in['msg_w'], 'L0_gnn_msg_b': _L0_gnn_in['msg_b'], 'L0_gnn_upd_w': _L0_gnn_in['upd_w'], 'L0_gnn_upd_b': _L0_gnn_in['upd_b'], 'L0_gnn_gate_w': _L0_gnn_in['gate_w'], 'L0_gnn_gate_b': _L0_gnn_in['gate_b']}

def reference(x, src, dst, edge_type_500, L0_gnn_relation_emb, L0_gnn_msg_w, L0_gnn_msg_b, L0_gnn_upd_w, L0_gnn_upd_b, L0_gnn_gate_w, L0_gnn_gate_b):
    import jax
    import jax.numpy as jnp

    def _L0_gnn_ref(h, edge_index, edge_type, relation_emb, msg_w, msg_b, upd_w, upd_b, gate_w, gate_b):
        import jax, jax.numpy as jnp
        import numpy as np
        G = (1.0, 1.0)

        def to_hypercomplex(x, n_blades):
            return x.reshape(*x.shape[:-1], n_blades, -1).swapaxes(-2, -1)

        def clifford_kernel_2d(w, g):
            g0, g1 = g
            k0 = jnp.concatenate([w[0], g0 * w[1], g1 * w[2], -g0 * g1 * w[3]], axis=1)
            k1 = jnp.concatenate([w[1], w[0], -g1 * w[3], g1 * w[2]], axis=1)
            k2 = jnp.concatenate([w[2], g0 * w[3], w[0], -g0 * w[1]], axis=1)
            k3 = jnp.concatenate([w[3], w[2], w[1], w[0]], axis=1)
            return jnp.concatenate([k0, k1, k2, k3], axis=0)

        def clifford_linear(x, w, b, g=G):
            N = x.shape[0]
            k = clifford_kernel_2d(w, g)
            xf = x.swapaxes(-2, -1).reshape(N, -1)
            out = xf @ k.T + b.reshape(-1)
            C_out = w.shape[1]
            return out.reshape(N, 4, C_out).swapaxes(-2, -1)
        n_blades = 4
        num_nodes = h.shape[0]
        h_hc = to_hypercomplex(h, n_blades)
        r_hc = to_hypercomplex(relation_emb, n_blades)
        src, dst = (edge_index[0], edge_index[1])
        h_src = h_hc[src]
        r_uv = r_hc[edge_type]
        m = clifford_linear(h_src * r_uv, msg_w, msg_b)
        gate = jax.nn.sigmoid(r_uv.reshape(r_uv.shape[0], -1) @ gate_w.T + gate_b)
        m = m * gate[:, :, None]
        ones = jnp.ones_like(src, dtype=jnp.float32)
        deg_src = jax.ops.segment_sum(ones, src, num_segments=num_nodes)
        deg_dst = jax.ops.segment_sum(ones, dst, num_segments=num_nodes)
        norm = jnp.maximum(deg_src[src] * deg_dst[dst], 1.0) ** (-0.5)
        m = m * norm[:, None, None]
        h_agg = jax.ops.segment_sum(m, dst, num_segments=num_nodes)
        h_out = clifford_linear(h_hc + h_agg, upd_w, upd_b)
        return h_out.reshape(num_nodes, -1)
    edge_index = jnp.stack([src, dst])
    h = jnp.maximum(_layernorm(x, axis=-1), 0.0)
    x = x + _L0_gnn_ref(h, edge_index, edge_type_500, L0_gnn_relation_emb, L0_gnn_msg_w, L0_gnn_msg_b, L0_gnn_upd_w, L0_gnn_upd_b, L0_gnn_gate_w, L0_gnn_gate_b)
    return x

_drawn_inputs = setup_inputs


def setup_inputs(seed=0):
    import zlib

    import numpy as np

    out = dict(_drawn_inputs(seed))
    spreads = {}
    factors = {'L0_gnn_msg_b': 3.162, 'L0_gnn_gate_w': 3.356}
    for name, (base, spread) in spreads.items():
        noise = np.random.default_rng([zlib.crc32(name.encode()), seed]).standard_normal(out[name].shape)
        drawn = base * np.exp(spread * noise) if base else spread * noise
        out[name] = jnp.asarray(drawn.astype(out[name].dtype))
    for name, factor in factors.items():
        out[name] = (out[name] * factor).astype(out[name].dtype)
    return out
```

```python
from contextlib import ExitStack

import concourse.bass as bass
from concourse import mybir

ALU = mybir.AluOpType
ACT = mybir.ActivationFunctionType
AX = mybir.AxisListType
F32 = mybir.dt.float32
F32R = mybir.dt.float32r
F16 = mybir.dt.float16
BF16 = mybir.dt.bfloat16
I32 = mybir.dt.int32
I16 = mybir.dt.int16
ds = bass.ds

P = 128
D = 256
C = 64
BL = 4
EPS = 1e-5
GRP = 4
BODY = 8
WIN = 128
PAD_ID = 16383
BLADE = [[0, 1, 2, 3], [1, 0, 3, 2], [2, 3, 0, 1], [3, 2, 1, 0]]
SIGN = [[1, 1, 1, -1], [1, 1, -1, 1], [1, 1, 1, -1], [1, 1, 1, 1]]


def at_least(eng, sem, value):
    if isinstance(value, int) and value <= 0:
        return
    eng.wait_ge(sem, value)


def hold(eng, passed):
    eng.sem_inc(passed, 1)


class Sizes:

    def __init__(self, n, e, r):
        self.N, self.E, self.R = n, e, r
        self.NT = -(-n // P)
        self.LAST = n - (self.NT - 1) * P
        self.NP = self.NT * P
        self.STEPS = -(-e // (P * BODY))
        self.CH = self.STEPS * BODY
        self.NG = self.CH // GRP
        self.NB = -(-self.CH // P)
        self.CB = self.CH - (self.NB - 1) * P
        self.FULL = e // P - (self.NB - 1) * P
        self.REST = e % P
        self.KT = -(-r // P)
        self.RL = r - (self.KT - 1) * P
        self.ACCW = self.NP + WIN
        self.DX = D + 1
        self.DM = D + 2
        self.PER = self.CH // 8 // self.NT * 8
        assert self.NT % 14 == 0 and self.NP <= 16000 and r <= 2048
        assert self.PER * self.NT == self.CH and 0 < self.FULL < P and self.KT > 1


def stage_1(nc, z, io, dram, t, x_in):
    ctx = ExitStack()
    with ctx:
        def sb(name, shape, dt):
            return ctx.enter_context(nc.sbuf_tensor(name, shape, dt))

        def sem(name):
            return ctx.enter_context(nc.semaphore(name))

        lists = ["src", "dst", "typ"]
        rows_i = [sb(f"rows_i_{n}", [P, z.NB, P], I32) for n in lists]
        rows_f = [r[:, :, :].bitcast(F32) for r in rows_i]
        rows_h = sb("rows_h", [P, z.NB, P], F16)
        cols = [sb(f"cols_{n}", [P, z.CH], F32) for n in lists]
        base = sb("base", [P, z.NG], F32)
        far, here = cols[0], cols[2]
        bad = sb("bad", [P, 1], F32)
        col16 = [sb(f"col16_{n}", [P, z.CH], I16) for n in ("dst", "typ")]
        upd_w = sb("upd_w", [P, C, BL], F32)
        msg_w = sb("msg_w", [P, BL, C], F32)
        msg_k = sb("msg_k", [P, 2, D], F32)
        msg_b = sb("msg_b", [P, 2], F32)
        rel = sb("rel", [P, z.KT, D], F32)
        gate_w = sb("gate_w", [P, D], F32)
        gate_b = sb("gate_b", [P, 1], F32)
        logit = sb("logit", [P, z.KT], F32)
        gate = sb("gate", [P, z.KT], F32)
        gated = sb("gated", [P, z.KT, z.DM], F32)
        prod = gated
        pt = [ctx.enter_context(nc.psum_tensor(f"turn{n}", [P, 512], F32)) for n in range(8)]

        pads_set = sem("pads_set")
        consts_set = sem("consts_set")
        iotas_set = sem("iotas_set")
        list_in = [sem(f"in_{n}") for n in lists]
        cast = sem("lists_cast")
        half_cast = sem("typ_half_cast")
        turned = sem("turned")
        unloaded = sem("turn_unloaded")
        cols_ready = sem("cols_ready")
        base_ps = sem("base_in_psum")
        chain = sem("vector_chain")
        bad_ready = sem("bad_ready")
        bad_ps = sem("bad_in_psum")
        w_in = sem("weights_in")
        w_built = sem("weights_built")
        w_ps = sem("weights_in_psum")
        rel_zero = sem("rel_zeroed")
        rel_in = sem("rel_in")
        logit_ready = sem("logit_ready")
        gate_ready = sem("gate_ready")
        gated_ready = sem("gated_ready")
        stored = sem("stage1_stored")
        x_zero = sem("x_zeroed")

        banks = [list(range(b, min(b + 4, z.NB))) for b in range(0, z.NB, 4)]
        assert len(banks) == 4

        with nc.Block() as block:
            @block.sync
            def _(sp):
                sp.wait_ge(pads_set, 3)
                for n, arr in enumerate((io["src"], io["dst"], io["typ"])):
                    full = (z.NB - 1) * P * P
                    sp.dma_start(rows_i[n][:, 0:z.NB - 1, :],
                                 arr[0:full].rearrange("(b p j) -> p b j", p=P, j=P)).then_inc(list_in[n], 16)
                    sp.dma_start(rows_i[n][0:z.FULL, z.NB - 1, :],
                                 arr[full:full + z.FULL * P].rearrange("(p j) -> p j", j=P)).then_inc(list_in[n], 16)
                    sp.dma_start(rows_i[n][z.FULL:z.FULL + 1, z.NB - 1, 0:z.REST],
                                 arr[z.E - z.REST:z.E].rearrange("(p j) -> p j", p=1)).then_inc(list_in[n], 16)
                for h in range(2):
                    sp.dma_start(upd_w[C * h:C * h + C, :, :], io["upd_w"]).then_inc(w_in, 16)
                    sp.dma_start(msg_w[C * h:C * h + C, :, :], io["msg_w"]).then_inc(w_in, 16)
                sp.dma_start(msg_b[:, :], io["msg_b"]).then_inc(w_in, 16)
                sp.dma_start(t["upd_b"][:, :], io["upd_b"]).then_inc(w_in, 16)
                sp.wait_ge(rel_zero, 1)
                sp.dma_start(rel[:, 0:z.KT - 1, :],
                             io["rel"][0:(z.KT - 1) * P, :].rearrange("(k p) d -> p k d", p=P)).then_inc(rel_in, 16)
                sp.dma_start(rel[0:z.RL, z.KT - 1, :], io["rel"][(z.KT - 1) * P:z.R, :]).then_inc(rel_in, 16)
                sp.dma_start(gate_w[:, :], io["gate_w"].to_broadcast((P, D))).then_inc(rel_in, 16)
                sp.dma_start(gate_b[:, :], io["gate_b"].to_broadcast((P, 1))).then_inc(rel_in, 16)
                sp.wait_ge(x_zero, 1)
                for c in range(0, z.NT - 14, 14):
                    sp.dma_start(t["x_all"][:, c:c + 14, :],
                                 io["x"][c * P:(c + 14) * P, :].rearrange("(t p) d -> p t d", p=P)).then_inc(x_in, 16)
                c = z.NT - 14
                sp.dma_start(t["x_all"][:, c:c + 13, :],
                             io["x"][c * P:(c + 13) * P, :].rearrange("(t p) d -> p t d", p=P)).then_inc(x_in, 16)
                sp.dma_start(t["x_all"][0:z.LAST, z.NT - 1, :], io["x"][z.NP - P:z.N, :]).then_inc(x_in, 16)

            @block.scalar
            def _(act):
                act.wait_ge(w_in, 96)
                upd_cols = t["upd_k"][:, :, :].rearrange("p h (c b) -> p h c b", b=BL)
                for i in range(BL):
                    for j in range(BL):
                        p0 = C * (j % 2)
                        nc.scalar.mul(upd_cols[p0:p0 + C, j // 2, :, i], upd_w[p0:p0 + C, :, BLADE[i][j]],
                                      float(SIGN[i][j])).then_inc(w_built, 1)
                        p0 = C * (i % 2)
                        nc.scalar.mul(msg_k[p0:p0 + C, i // 2, C * j:C * j + C], msg_w[p0:p0 + C, BLADE[i][j], :],
                                      float(SIGN[i][j])).then_inc(w_built, 1)
                act.wait_ge(logit_ready, 1)
                nc.scalar.activation(gate[:, :], logit[:, :], ACT.Sigmoid, bias=gate_b[:, :]).then_inc(gate_ready, 1)
                act.wait_ge(half_cast, 1)
                act.dma_start(dram["typ_row"].rearrange("(b p j) -> p b j", p=P, j=P), rows_h[:, :, :]).then_inc(stored, 16)
                act.wait_ge(cols_ready, 2)
                act.dma_start(dram["dst_cols"], col16[0][:, :]).then_inc(stored, 16)
                act.dma_start(dram["typ_cols"], col16[1][:, :]).then_inc(stored, 16)
                act.wait_ge(gated_ready, 2 * z.KT + 1)
                act.dma_start(dram["rg_tab"][0:(z.KT - 1) * P, :].rearrange("(k p) d -> p k d", p=P),
                              gated[:, 0:z.KT - 1, 0:z.DX]).then_inc(stored, 16)
                act.dma_start(dram["rg_tab"][(z.KT - 1) * P:z.R, :],
                              gated[0:z.RL, z.KT - 1, 0:z.DX]).then_inc(stored, 16)
                act.wait_ge(stored, 80)

            @block.gpsimd
            def _(pool):
                for n in range(3):
                    nc.gpsimd.memset(rows_i[n][:, z.NB - 1, :], PAD_ID).then_inc(pads_set, 1)
                nc.gpsimd.memset(rel[:, z.KT - 1, :], 0.0).then_inc(rel_zero, 1)
                nc.gpsimd.memset(t["x_all"][:, z.NT - 1, :], 0.0).then_inc(x_zero, 1)
                nc.gpsimd.memset(t["ident"][:, :], 0.0).then_inc(consts_set, 1)
                nc.gpsimd.memset(t["ones"][:, :], 1.0).then_inc(consts_set, 1)
                nc.gpsimd.memset(t["eps"][:, :], EPS).then_inc(consts_set, 1)
                pool.wait_ge(consts_set, 1)
                nc.gpsimd.affine_select(out=t["ident"][:, :], in_=t["ident"][:, :], compare_op=ALU.not_equal, fill=1.0,
                                        base=0, pattern=[[-1, P]], channel_multiplier=1).then_inc(iotas_set, 1)
                nc.gpsimd.iota(t["iota"][:, :], [[1, P]], base=0, channel_multiplier=0,
                               allow_small_or_imprecise_dtypes=True).then_inc(iotas_set, 1)
                nc.gpsimd.iota(t["iota_b"][:, :], [[1, P]], base=0, channel_multiplier=0,
                               allow_small_or_imprecise_dtypes=True).then_inc(iotas_set, 1)
                nc.gpsimd.iota(t["rel_id"][:, :], [[P, z.KT]], base=0, channel_multiplier=1,
                               allow_small_or_imprecise_dtypes=True).then_inc(iotas_set, 1)

            @block.tensor
            def _(pe):
                pe.wait_ge(iotas_set, 1)
                pe.wait_ge(consts_set, 2)
                for n in range(3):
                    pe.wait_ge(cast, n + 1)
                    for b, blocks in enumerate(banks):
                        if n == 2:
                            pe.wait_ge(unloaded, b + 1)
                        for k, blk in enumerate(blocks):
                            rows = P if blk < z.NB - 1 else z.CB
                            mm = nc.tensor.transpose(pt[4 * (n % 2) + b][:, k * P:k * P + rows],
                                                     rows_f[n][0:rows, blk, :], t["ident"][0:rows, 0:rows])
                        mm.then_inc(turned, 1)
                pe.wait_ge(unloaded, 8)
                nc.tensor.matmul(pt[4][:, 0:z.NG], t["ones"][0:1, :], cols[1][0:1, 0:z.CH:GRP],
                                 start=True, stop=True).then_inc(base_ps, 1)
                pe.wait_ge(w_built, 2 * BL * BL)
                for i in range(2):
                    for m in range(2):
                        nc.tensor.matmul(pt[5][:, i * D:i * D + D], msg_k[:, m, i * P:i * P + P], t["upd_k"][:, m, :],
                                         start=(m == 0), stop=(m == 1))
                for m in range(2):
                    mm = nc.tensor.matmul(pt[6][0:1, 0:D], msg_b[:, m:m + 1], t["upd_k"][:, m, :],
                                          start=(m == 0), stop=(m == 1))
                mm.then_inc(w_ps, 1)
                pe.wait_ge(bad_ready, 1)
                nc.tensor.matmul(pt[7][0:1, 0:1], bad[:, :], t["ones"][:, 0:1], start=True, stop=True).then_inc(bad_ps, 1)

            @block.vector
            def _(dve):
                links = [0]

                def link(ins):
                    links[0] += 1
                    ins.then_inc(chain, 1)
                    dve.wait_ge(chain, links[0])

                for n in range(3):
                    dve.wait_ge(list_in[n], 48)
                    nc.vector.tensor_copy(rows_f[n], rows_i[n][:, :, :]).then_inc(cast, 1)
                dve.wait_ge(cast, 3)
                nc.vector.tensor_copy(rows_h[:, :, :], rows_f[2]).then_inc(half_cast, 1)
                dve.wait_ge(rel_in, 64)
                for k in range(z.KT):
                    nc.vector.tensor_tensor(prod[:, k, 0:D], rel[:, k, :], gate_w[:, :], ALU.mult).then_inc(chain, 1)
                links[0] += z.KT
                dve.wait_ge(chain, links[0])
                nc.vector.tensor_reduce(logit[:, :], prod[:, :, 0:D], AX.X, ALU.add).then_inc(logit_ready, 1)

                def unload(n):
                    for b, blocks in enumerate(banks):
                        dve.wait_ge(turned, 4 * n + b + 1)
                        width = min(4 * P, z.CH - b * 4 * P)
                        nc.vector.tensor_copy(cols[n][:, b * 4 * P:b * 4 * P + width],
                                              pt[4 * (n % 2) + b][:, 0:width]).then_inc(unloaded, 1)

                unload(0)
                dve.wait_ge(unloaded, 4)
                nc.vector.tensor_scalar(t["src16"][:, :], cols[0][:, :], float(z.N - 1), None, ALU.min).then_inc(chain, 1)
                links[0] += 1
                link(nc.vector.tensor_copy(t["src_lo"][:, :], cols[0][:, :]))
                nc.vector.tensor_scalar(t["src_hi"][:, :], t["src_lo"][:, :], 7, None, ALU.arith_shift_right).then_inc(chain, 1)
                links[0] += 1
                dve.wait_ge(chain, links[0])
                link(nc.vector.tensor_scalar(t["src_lo"][:, :], t["src_lo"][:, :], P - 1, None, ALU.bitwise_and))
                unload(1)
                unload(2)
                dve.wait_ge(unloaded, 12)
                nc.vector.tensor_copy(col16[0][:, :], cols[1][:, :]).then_inc(cols_ready, 1)
                nc.vector.tensor_scalar(col16[1][:, :], cols[2][:, :], float(z.R - 1), None, ALU.min).then_inc(cols_ready, 1)
                dve.wait_ge(cols_ready, 2)
                nc.vector.tensor_copy(t["typ16"][:, :, :],
                                      col16[1][:, :].rearrange("p (s c) -> p s c", c=BODY)[:, :, BODY - 2:BODY]).then_inc(chain, 1)
                links[0] += 1
                dve.wait_ge(base_ps, 1)
                link(nc.vector.tensor_scalar(base[:, :], pt[4][:, 0:z.NG], float(z.NP), 0.0, ALU.min, ALU.max))
                nc.vector.tensor_copy(t["base_id"][:, :], base[0:1, :]).then_inc(chain, 1)
                links[0] += 1
                link(nc.vector.tensor_tensor(far[:, :].rearrange("p (g k) -> p g k", k=GRP),
                                             cols[1][:, :].rearrange("p (g k) -> p g k", k=GRP),
                                             base[:, :].to_broadcast((P, z.NG, GRP)), ALU.subtract))
                nc.vector.tensor_copy(t["rel16"][:, :], far[:, :]).then_inc(chain, 1)
                links[0] += 1
                link(nc.vector.tensor_scalar(here[:, :], cols[1][:, :], float(PAD_ID), None, ALU.is_lt))
                nc.vector.tensor_scalar(cols[1][:, :], far[:, :], 0.0, None, ALU.is_lt).then_inc(chain, 1)
                links[0] += 1
                link(nc.vector.tensor_scalar(far[:, :], far[:, :], float(WIN), None, ALU.is_ge))
                link(nc.vector.tensor_tensor(far[:, :], far[:, :], here[:, :], ALU.mult))
                link(nc.vector.tensor_tensor(far[:, :], far[:, :], cols[1][:, :], ALU.add))
                nc.vector.tensor_reduce(bad[:, :], far[:, :], AX.X, ALU.add).then_inc(bad_ready, 1)
                dve.wait_ge(gate_ready, 1)
                for k in range(z.KT):
                    nc.vector.tensor_scalar(gated[:, k, 0:D], rel[:, k, :], gate[:, k:k + 1], None,
                                            ALU.mult).then_inc(gated_ready, 1)
                    nc.vector.tensor_copy(gated[:, k, D:D + 1], gate[:, k:k + 1]).then_inc(gated_ready, 1)
                nc.vector.memset(gated[:, :, D + 1:D + 2], 0.0).then_inc(gated_ready, 1)
                dve.wait_ge(gated_ready, 2 * z.KT + 1)
                link(nc.vector.tensor_copy(t["table"][:, :, 0, :], gated[:, :, :]))
                link(nc.vector.tensor_tensor(t["table"][:, :, 1, :], gated[:, :, :],
                                             t["table"][:, :, 0, :].bitcast(F32), ALU.subtract))
                link(nc.vector.memset(t["w_ext"][:, :], 0.0))
                dve.wait_ge(w_ps, 1)
                link(nc.vector.tensor_copy(t["w_agg"][:, :, :], pt[5][:, :].rearrange("p (h d) -> p h d", h=2)))
                link(nc.vector.tensor_copy(t["w_ext"][0:1, 0:D], pt[6][0:1, 0:D]))
                link(nc.vector.tensor_copy(t["w_ext"][:, D:D + 1], t["ident"][0:2, 1:2]))
                dve.wait_ge(bad_ps, 1)
                link(nc.vector.tensor_copy(t["flag"][:, :], pt[7][0:1, 0:1]))


def stage_2(nc, z, dram, t, x_in, s2):
    ctx = ExitStack()
    with ctx:
        def sb(name, shape, dt):
            return ctx.enter_context(nc.sbuf_tensor(name, shape, dt))

        def sem(name):
            return ctx.enter_context(nc.semaphore(name))

        SLOT = 8
        SLOTS = 2 * z.PER // SLOT
        HI = z.NT
        one_lo = sb("one_lo", [P, SLOTS, SLOT, P], BF16)
        one_hi = sb("one_hi", [P, SLOTS, SLOT, HI], BF16)
        zero_b = sb("zero_b", [P, P], BF16)
        stats = sb("stats", [P, z.NT, 6], F32)
        mean = sb("mean", [P, z.NT], F32)
        half = sb("half", [P, z.NT], F32)
        var = sb("var", [P, z.NT], F32)
        std = sb("std", [P, z.NT], F32)
        h = sb("h", [P, 2, D], F32)
        h_t = sb("h_t", [P, 2, D], F32)
        base_row = sb("base_row", [P, 2, D], F32)
        deg = sb("deg", [P, z.NT], F32)
        ps_turn = [ctx.enter_context(nc.psum_tensor(f"ps_turn{n}", [P, 512], F32)) for n in range(2)]
        ps_out = [ctx.enter_context(nc.psum_tensor(f"ps_out{n}", [P, 512], F32)) for n in range(2)]
        ps_deg = ctx.enter_context(nc.psum_tensor("ps_deg", [P, 512], F32))

        stats_ready = sem("stats_ready")
        moments = sem("moments")
        var_ready = sem("var_ready")
        std_ready = sem("std_ready")
        norm_ready = sem("norm_ready")
        onehots = sem("onehots_ready")
        counted = sem("onehots_counted")
        h_ready = [sem(f"h_ready{n}") for n in range(2)]
        turned = [sem(f"h_turned{n}") for n in range(2)]
        t_ready = [sem(f"h_t_ready{n}") for n in range(2)]
        summed = [sem(f"row_summed{n}") for n in range(2)]
        row_ready = [sem(f"row_ready{n}") for n in range(2)]
        row_out = [sem(f"row_stored{n}") for n in range(2)]
        zeros = sem("zeros_ready")
        deg_done = sem("deg_done")
        deg_ready = sem("deg_clamped")
        root_ready = sem("deg_root_ready")
        link2 = sem("stage2_chain")
        passed = sem("stage2_sp_passed")
        STEP = 2
        N_STEPS = z.NT // STEP

        with nc.Block() as block:
            @block.sync
            def _(sp):
                def step(i):
                    for s in range(STEP):
                        sp.wait_ge(row_ready[s], i + 1)
                        hold(sp, passed)
                        sp.dma_start(dram["base_out"][ds((i * STEP + s) * P, P), :], base_row[:, s, :]).then_inc(row_out[s], 16)

                with sp.Fori(0, N_STEPS) as i:
                    step(i)
                for s in range(STEP):
                    sp.wait_ge(row_out[s], 16 * N_STEPS)

            @block.scalar
            def _(act):
                act.wait_ge(var_ready, 1)
                nc.scalar.activation(std[:, :], var[:, :], ACT.Sqrt, bias=t["eps"][:, :]).then_inc(std_ready, 1)
                act.wait_ge(norm_ready, 2)

                def step(i):
                    for s in range(STEP):
                        tile = i * STEP + s
                        at_least(act, turned[s], i)
                        nc.scalar.activation(h[:, s, :].rearrange("p (a d) -> p a d", a=1), t["x_all"][:, ds(tile, 1), :],
                                             ACT.Relu, bias=t["shift"][:, ds(tile, 1)],
                                             scale=t["rstd"][:, ds(tile, 1)]).then_inc(h_ready[s], 1)
                    for s in range(STEP):
                        act.wait_ge(turned[s], i + 1)
                        at_least(act, summed[s], i)
                        nc.scalar.copy(h_t[:, s, :], ps_turn[s][:, 0:D]).then_inc(t_ready[s], 1)
                    for s in range(STEP):
                        act.wait_ge(summed[s], i + 1)
                        at_least(act, row_out[s], 16 * i)
                        nc.scalar.copy(base_row[:, s, :], ps_out[s][:, 0:D]).then_inc(row_ready[s], 1)

                step(0)
                with act.Fori(1, N_STEPS) as i:
                    step(i)
                act.wait_ge(deg_ready, 1)
                nc.scalar.activation(deg[:, :], deg[:, :], ACT.Sqrt).then_inc(root_ready, 1)

            @block.tensor
            def _(pe):
                pe.wait_ge(zeros, 1)
                nc.tensor.matmul(ps_deg[:, 0:HI], zero_b[:, :], zero_b[:, 0:HI], start=True, stop=False)

                def count(n, b):
                    pe.wait_ge(onehots, n + 1)
                    for k in range(SLOT):
                        mm = nc.tensor.matmul(ps_deg[:, 0:HI], one_lo[:, b, k, :], one_hi[:, b, k, :],
                                              start=False, stop=False)
                    mm.then_inc(counted, 1)

                def step(i):
                    for s in range(STEP):
                        pe.wait_ge(h_ready[s], i + 1)
                        at_least(pe, t_ready[s], i)
                        for a in range(2):
                            mm = nc.tensor.transpose(ps_turn[s][:, a * P:a * P + P], h[:, s, a * P:a * P + P], t["ident"][:, :])
                        mm.then_inc(turned[s], 1)
                        count(i * SLOTS + s, s)
                    for s in range(STEP):
                        pe.wait_ge(t_ready[s], i + 1)
                        at_least(pe, row_ready[s], i)
                        nc.tensor.matmul(ps_out[s][:, 0:D], t["ones"][0:1, :], t["upd_b"][:, :], start=True, stop=False)
                        for a in range(2):
                            nc.tensor.matmul(ps_out[s][:, 0:D], h_t[:, s, a * P:a * P + P], t["upd_k"][:, a, :],
                                             start=False, stop=False)
                        nc.tensor.matmul(ps_out[s][:, 0:D], t["ident"][:, :],
                                         t["x_all"][:, ds(i * STEP + s, 1), :].rearrange("p a d -> p (a d)"),
                                         start=False, stop=True).then_inc(summed[s], 1)
                        count(i * SLOTS + STEP + s, STEP + s)

                step(0)
                with pe.Fori(1, N_STEPS) as i:
                    step(i)
                nc.tensor.matmul(ps_deg[:, 0:HI], zero_b[:, :], zero_b[:, 0:HI], start=False, stop=True).then_inc(deg_done, 1)

            @block.vector
            def _(dve):
                nc.vector.memset(zero_b[:, :], 0.0).then_inc(zeros, 1)
                dve.wait_ge(x_in, 16 * (z.NT // 14 + 1))
                with dve.Fori(0, z.NT) as i:
                    nc.vector.bn_stats(stats[:, ds(i, 1), :].rearrange("p a c -> p (a c)"),
                                       t["x_all"][:, ds(i, 1), :].rearrange("p a d -> p (a d)")).then_inc(stats_ready, 1)
                dve.wait_ge(stats_ready, z.NT)
                nc.vector.tensor_tensor(mean[:, :], stats[:, :, 1], stats[:, :, 4], ALU.add).then_inc(moments, 1)
                nc.vector.tensor_tensor(half[:, :], stats[:, :, 1], stats[:, :, 4], ALU.subtract).then_inc(moments, 1)
                nc.vector.tensor_tensor(var[:, :], stats[:, :, 2], stats[:, :, 5], ALU.add).then_inc(moments, 1)
                dve.wait_ge(moments, 2)
                nc.vector.scalar_tensor_tensor(out=half[:, :], in0=half[:, :], scalar=0.25, in1=half[:, :],
                                               op0=ALU.mult, op1=ALU.mult).then_inc(moments, 1)
                dve.wait_ge(moments, 4)
                nc.vector.scalar_tensor_tensor(out=var[:, :], in0=var[:, :], scalar=1.0 / D, in1=half[:, :],
                                               op0=ALU.mult, op1=ALU.add).then_inc(var_ready, 1)
                dve.wait_ge(std_ready, 1)
                nc.vector.reciprocal(t["rstd"][:, :], std[:, :]).then_inc(norm_ready, 1)
                dve.wait_ge(norm_ready, 1)
                nc.vector.scalar_tensor_tensor(out=t["shift"][:, :], in0=mean[:, :], scalar=-0.5, in1=t["rstd"][:, :],
                                               op0=ALU.mult, op1=ALU.mult).then_inc(norm_ready, 1)

                def step(i):
                    for b in range(SLOTS):
                        at_least(dve, counted, i * SLOTS + b + 1 - SLOTS)
                        for k in range(SLOT):
                            c = (i * SLOTS + b) * SLOT + k
                            nc.vector.tensor_scalar(one_lo[:, b, k, :], t["iota_b"][:, :], t["src_lo"][:, ds(c, 1)], None,
                                                    ALU.is_equal)
                            last = nc.vector.tensor_scalar(one_hi[:, b, k, :], t["iota_b"][:, 0:HI],
                                                           t["src_hi"][:, ds(c, 1)], None, ALU.is_equal)
                        last.then_inc(onehots, 1)

                step(0)
                with dve.Fori(1, N_STEPS) as i:
                    step(i)
                dve.wait_ge(deg_done, 1)
                nc.vector.tensor_scalar(deg[:, :], ps_deg[:, 0:HI], 1.0, None, ALU.max).then_inc(deg_ready, 1)
                dve.wait_ge(root_ready, 1)
                nc.vector.reciprocal(t["src_norm"][:, :], deg[:, :]).then_inc(link2, 1)
                dve.wait_ge(link2, 1)
                nc.vector.tensor_tensor(t["rstd"][:, :], t["rstd"][:, :], t["src_norm"][:, :], ALU.mult).then_inc(link2, 1)
                nc.vector.tensor_tensor(t["shift"][:, :], t["shift"][:, :], t["src_norm"][:, :], ALU.mult).then_inc(link2, 1)


def stage_3(nc, z, dram, t):
    ctx = ExitStack()
    with ctx:
        def sem(name):
            return ctx.enter_context(nc.semaphore(name))

        LOT = 7
        BY_ACT = 5
        rows = [ctx.enter_context(nc.sbuf_tensor(f"hs_rows{s}", [P, LOT, z.DX], F32)) for s in range(2)]
        act_done = [sem(f"hs_act{s}") for s in range(2)]
        dve_half = [sem(f"hs_scaled{s}") for s in range(2)]
        dve_done = [sem(f"hs_dve{s}") for s in range(2)]
        passed = sem("stage3_sp_passed")
        out = [sem(f"hs_stored{s}") for s in range(2)]
        STEPS = z.NT // (2 * LOT)

        with nc.Block() as block:
            @block.sync
            def _(sp):
                with sp.Fori(0, STEPS) as i:
                    for s in range(2):
                        sp.wait_ge(act_done[s], (i + 1) * BY_ACT)
                        hold(sp, passed)
                        sp.wait_ge(dve_done[s], (i + 1) * 2)
                        hold(sp, passed)
                        sp.dma_start(dram["h_tab"][ds((i * 2 + s) * (LOT * P), LOT * P), :].rearrange("(t p) d -> p t d", p=P),
                                     rows[s][:, :, :]).then_inc(out[s], 16)
                for s in range(2):
                    sp.wait_ge(out[s], 16 * STEPS)

            @block.scalar
            def _(act):
                def step(i):
                    for s in range(2):
                        at_least(act, out[s], 16 * i)
                        for k in range(BY_ACT):
                            tile = (i * 2 + s) * LOT + k
                            nc.scalar.activation(rows[s][:, k:k + 1, 0:D], t["x_all"][:, ds(tile, 1), :],
                                                 ACT.Relu, bias=t["shift"][:, ds(tile, 1)],
                                                 scale=t["rstd"][:, ds(tile, 1)]).then_inc(act_done[s], 1)
                step(0)
                with act.Fori(1, STEPS) as i:
                    step(i)

            @block.vector
            def _(dve):
                def step(i):
                    for s in range(2):
                        at_least(dve, out[s], 16 * i)
                        for k in range(BY_ACT, LOT):
                            tile = (i * 2 + s) * LOT + k
                            nc.vector.tensor_scalar(rows[s][:, k:k + 1, 0:D], t["x_all"][:, ds(tile, 1), :],
                                                    t["rstd"][:, ds(tile, 1)], t["shift"][:, ds(tile, 1)],
                                                    ALU.mult, ALU.add).then_inc(dve_half[s], 1)
                        nc.vector.tensor_copy(rows[s][:, :, D], t["src_norm"][:, ds((i * 2 + s) * LOT, LOT)]).then_inc(dve_done[s], 1)
                        dve.wait_ge(dve_half[s], (i + 1) * (LOT - BY_ACT))
                        nc.vector.tensor_scalar(rows[s][:, BY_ACT:LOT, 0:D], rows[s][:, BY_ACT:LOT, 0:D], 0.0, None,
                                                ALU.max).then_inc(dve_done[s], 1)
                step(0)
                with dve.Fori(1, STEPS) as i:
                    step(i)


def stage_4(nc, z, dram, t):
    ctx = ExitStack()
    with ctx:
        def sb(name, shape, dt):
            return ctx.enter_context(nc.sbuf_tensor(name, shape, dt))

        def sem(name):
            return ctx.enter_context(nc.semaphore(name))

        PAIRS = BODY // 2
        ORDER = [0, 1, 3, 2]
        PLACE = {0: 0, 1: 1, 3: 0, 2: 1}
        BEFORE = {3: 0, 2: 1}
        hrow = sb("hrow", [P, BODY, z.DX], F32)
        rrow = sb("rrow", [P, 2, z.DX], F32)
        msg = sb("msg", [P, 4, z.DM], F32)
        member = sb("member", [P, 4, WIN], F32)
        typ_b = [sb(f"typ_b{g}", [P, (4, 2)[g] * P], F16) for g in range(2)]
        one = [sb(f"one{g}", [P, z.KT, (4, 2)[g] * P], F32R) for g in range(2)]
        part = sb("part", [P, 2, z.DM], F32)
        idx_a = sb("idx_a", [P, 4], I32)
        idx_b = sb("idx_b", [P, 6], I32)
        dst_g = sb("dst_g", [P, GRP], I16)
        typ_g = sb("typ_g", [P, GRP], I16)
        place_g = sb("place_g", [P, GRP], F32)
        idx_g = sb("idx_g", [P, 2 * GRP], I32)
        ps_rel = [ctx.enter_context(nc.psum_tensor(f"ps_rel{n}", [P, 2, 512], F32)) for n in range(2)]
        ps_sum = [ctx.enter_context(nc.psum_tensor(f"ps_sum{n}", [P, 512], F32)) for n in range(2)]
        ps_tr = [ctx.enter_context(nc.psum_tensor(f"ps_tr{n}", [P, 512], F32)) for n in range(2)]

        ready = sem("msg_ones_set")
        zeroed = sem("acc_zeroed")
        idx_ready = [sem(f"idx_ready_{n}") for n in "ab"]
        h_in = [sem(f"hrow_in{k}") for k in range(BODY)]
        r_in = [sem(f"rrow_in{k}") for k in range(2)]
        typ_in = [sem(f"typ_in{g}") for g in range(2)]
        one_ready = [sem(f"one_ready{g}") for g in range(2)]
        rel_ready = [sem(f"rel_ready{q}") for q in range(PAIRS)]
        msg_ready = [sem(f"msg_ready{q}") for q in range(PAIRS)]
        msg_used = [sem(f"msg_used{q}") for q in range(PAIRS)]
        part_ready = [sem(f"part_ready{g}") for g in range(2)]
        part_turned = [sem(f"part_turned{g}") for g in range(2)]
        added = [sem(f"added{g}") for g in range(2)]
        g_in, g_set, g_rows, g_msg, g_place, g_member, g_sum, g_part, g_turned, g_added = (
            sem(n) for n in ("g_in", "g_set", "g_rows", "g_msg", "g_place", "g_member", "g_sum", "g_part",
                             "g_turned", "g_added"))
        passed = [sem(f"passed_{n}") for n in ("pool", "sp", "dve")]
        L = z.STEPS - 1
        PSUM_OF = {0: 0, 1: 1, 2: 0}

        def fast_or_general(eng, fast, general):
            outside = eng.value_load(t["flag"][0:1, 0:1], min_val=0, max_val=z.CH * P)
            with eng.If(outside == 0):
                fast()
            with eng.Else():
                general()

        def over_steps(eng, step):
            step(0, True, False)
            with eng.Fori(1, L) as i:
                step(i, False, False)
            step(L, False, True)

        with nc.Block() as block:
            @block.sync
            def _(sp):
                def load(i, g):
                    at_least(sp, one_ready[g], i)
                    hold(sp, passed[1])
                    n = (4, 2)[g] * P
                    sp.dma_start(typ_b[g][:, :], dram["typ_row"][ds(i * (BODY * P) + g * GRP * P, n)].rearrange(
                        "(a n) -> a n", a=1).to_broadcast((P, n))).then_inc(typ_in[g], 16)

                def fast():
                    load(0, 0)
                    load(0, 1)
                    with sp.Fori(1, z.STEPS) as i:
                        load(i, 0)
                        load(i, 1)

                def general():
                    def group(g):
                        at_least(sp, g_set, g)
                        hold(sp, passed[1])
                        sp.dma_start(dst_g[:, :], dram["dst_cols"][:, ds(g * GRP, GRP)]).then_inc(g_in, 16)
                        sp.dma_start(typ_g[:, :], dram["typ_cols"][:, ds(g * GRP, GRP)]).then_inc(g_in, 16)
                    group(0)
                    with sp.Fori(1, z.NG) as g:
                        group(g)

                fast_or_general(sp, fast, general)

            @block.gpsimd
            def _(pool):
                def gather(rows, table, index, landed):
                    nc.gpsimd.indirect_dma_start(rows, None, dram[table], bass.IndirectOffsetOnAxis(ap=index, axis=0)
                                                 ).then_inc(landed, 16)

                def fast():
                    def step(i):
                        for q in ORDER:
                            if q in (0, 3):
                                pool.wait_ge(idx_ready[q // 3], i + 1)
                            at_least(pool, msg_ready[q], i)
                            hold(pool, passed[0])
                            for k in (2 * q, 2 * q + 1):
                                index = idx_a[:, k:k + 1] if q < 2 else idx_b[:, k - 4:k - 3]
                                gather(hrow[:, k, :], "h_tab", index, h_in[k])
                                if q == 3:
                                    gather(rrow[:, k - 6, :], "rg_tab", idx_b[:, k - 2:k - 1], r_in[k - 6])
                    step(0)
                    with pool.Fori(1, z.STEPS) as i:
                        step(i)

                def general():
                    with pool.Fori(0, z.NG) as g:
                        pool.wait_ge(g_set, g + 1)
                        hold(pool, passed[0])
                        for k in range(GRP):
                            gather(hrow[:, k, :], "h_tab", idx_g[:, k:k + 1], g_rows)
                            gather(hrow[:, GRP + k, :], "rg_tab", idx_g[:, GRP + k:GRP + k + 1], g_rows)

                fast_or_general(pool, fast, general)

            @block.scalar
            def _(act):
                def fast():
                    def indices(i, half):
                        if half == 0:
                            nc.scalar.copy(idx_a[:, :], t["src16"][:, ds(i * BODY, 4)]).then_inc(idx_ready[0], 1)
                        else:
                            nc.scalar.copy(idx_b[:, 0:4], t["src16"][:, ds(i * BODY + 4, 4)])
                            nc.scalar.copy(idx_b[:, 4:6].rearrange("p (a c) -> p a c", a=1),
                                           t["typ16"][:, ds(i, 1), :]).then_inc(idx_ready[1], 1)

                    def unload(i, g):
                        for q in (2 * g, 2 * g + 1):
                            act.wait_ge(msg_used[q], i + 1)
                        at_least(act, part_turned[g], i)
                        nc.scalar.copy(part[:, g, :], ps_sum[g][:, 0:z.DM]).then_inc(part_ready[g], 1)

                    def step(i, first, last):
                        if not first:
                            unload(i - 1, 1)
                        if not last:
                            for k in range(4):
                                act.wait_ge(h_in[k], 16 * i + 16)
                            indices(i + 1, 0)
                        unload(i, 0)
                        if not last:
                            for k in range(4, BODY):
                                act.wait_ge(h_in[k], 16 * i + 16)
                            for k in range(2):
                                act.wait_ge(r_in[k], 16 * i + 16)
                            indices(i + 1, 1)

                    indices(0, 0)
                    indices(0, 1)
                    over_steps(act, step)
                    unload(L, 1)

                def general():
                    with act.Fori(0, z.NG * z.NT) as u:
                        act.wait_ge(g_sum, u + 1)
                        nc.scalar.copy(part[:, 0, :], ps_sum[0][:, 0:z.DM]).then_inc(g_part, 1)

                fast_or_general(act, fast, general)

            def turn(pe, g):
                for a in range(2):
                    nc.tensor.transpose(ps_tr[g][:, a * P:a * P + P], part[:, g, a * P:a * P + P], t["ident"][:, :])
                return nc.tensor.transpose(ps_tr[g][0:2, D:D + P], part[:, g, D:z.DM], t["ident"][:, :])

            @block.tensor
            def _(pe):
                def fast():
                    def relate(i, q):
                        g = q // 2
                        if q in (0, 2):
                            pe.wait_ge(one_ready[g], i + 1)
                        if q == 2:
                            pe.wait_ge(msg_ready[0], i + 1)
                        else:
                            at_least(pe, msg_ready[2 - q] if q == 0 else msg_ready[1], i)
                        for c in range(2):
                            for k in range(z.KT):
                                for a in range(2):
                                    mm = nc.tensor.matmul(
                                        ps_rel[PSUM_OF[q]][:, c, 0:z.DM],
                                        one[g][:, k, ((q % 2) * 2 + c) * P:((q % 2) * 2 + c + 1) * P],
                                        t["table"][:, k, a, :], start=(k == 0 and a == 0), stop=(k == z.KT - 1 and a == 1))
                        mm.then_inc(rel_ready[q], 1)

                    def add(i, q, first, last):
                        g = q // 2
                        pe.wait_ge(msg_ready[q], i + 1)
                        if first:
                            at_least(pe, part_ready[g], i)
                        for c in range(2):
                            slot = 2 * PLACE[q] + c
                            mm = nc.tensor.matmul(ps_sum[g][:, 0:z.DM], member[:, slot, :], msg[:, slot, :],
                                                  start=(first and c == 0), stop=(last and c == 1))
                        mm.then_inc(msg_used[q], 1)

                    def turned(i, g):
                        pe.wait_ge(part_ready[g], i + 1)
                        at_least(pe, added[g], i)
                        turn(pe, g).then_inc(part_turned[g], 1)

                    def step(i, first, last):
                        relate(i, 0)
                        if not first:
                            turned(i - 1, 1)
                        relate(i, 1)
                        add(i, 0, True, False)
                        relate(i, 2)
                        add(i, 1, False, True)
                        add(i, 3, True, False)
                        turned(i, 0)
                        add(i, 2, False, True)

                    over_steps(pe, step)
                    turned(L, 1)

                def general():
                    with pe.Fori(0, z.NG * z.NT) as u:
                        pe.wait_ge(g_member, u + 1)
                        for k in range(GRP):
                            mm = nc.tensor.matmul(ps_sum[0][:, 0:z.DM], member[:, k, :], msg[:, k, :],
                                                  start=(k == 0), stop=(k == GRP - 1))
                        mm.then_inc(g_sum, 1)
                        pe.wait_ge(g_part, u + 1)
                        turn(pe, 0).then_inc(g_turned, 1)

                fast_or_general(pe, fast, general)

            @block.vector
            def _(dve):
                nc.vector.memset(msg[:, :, z.DM - 1:z.DM], 1.0).then_inc(ready, 1)
                nc.vector.memset(t["acc"][:, :, :], 0.0).then_inc(zeroed, 1)
                nc.vector.memset(t["acc_ext"][:, :], 0.0).then_inc(zeroed, 1)
                dve.wait_ge(ready, 1)
                dve.wait_ge(zeroed, 2)

                def add_window(g, at, done):
                    nc.vector.tensor_tensor(t["acc"][:, :, ds(at, WIN)], ps_tr[g][:, 0:D].rearrange("p (a n) -> p a n", a=2),
                                            t["acc"][:, :, ds(at, WIN)], ALU.add).then_inc(done, 1)
                    nc.vector.tensor_tensor(t["acc_ext"][:, ds(at, WIN)], ps_tr[g][0:2, D:D + P],
                                            t["acc_ext"][:, ds(at, WIN)], ALU.add).then_inc(done, 1)

                def fast():
                    def onehots(i, g):
                        dve.wait_ge(typ_in[g], 16 * i + 16)
                        at_least(dve, rel_ready[g + 1], i)
                        for k in range(z.KT):
                            last = nc.vector.tensor_scalar(one[g][:, k, :], typ_b[g][:, :], t["rel_id"][:, k:k + 1], None,
                                                           ALU.is_equal)
                        last.then_inc(one_ready[g], 1)

                    def messages(i, q):
                        place = 2 * PLACE[q]
                        if q in BEFORE:
                            dve.wait_ge(msg_used[BEFORE[q]], i + 1)
                        else:
                            at_least(dve, msg_used[3 - q], i)
                        for c in range(2):
                            nc.vector.tensor_scalar(member[:, place + c, :], t["iota"][:, :],
                                                    t["rel16"][:, ds(i * BODY + 2 * q + c, 1)], None, ALU.is_equal)
                        for k in (2 * q, 2 * q + 1):
                            dve.wait_ge(h_in[k], 16 * i + 16)
                        if q == 3:
                            for k in range(2):
                                dve.wait_ge(r_in[k], 16 * i + 16)
                            factor = rrow[:, :, :]
                        else:
                            dve.wait_ge(rel_ready[q], i + 1)
                            factor = ps_rel[PSUM_OF[q]][:, :, 0:z.DX]
                        nc.vector.tensor_tensor(msg[:, place:place + 2, 0:z.DX], factor, hrow[:, 2 * q:2 * q + 2, :],
                                                ALU.mult).then_inc(msg_ready[q], 1)

                    def add(i, g):
                        at = dve.value_load(t["base_id"][0:1, ds(2 * i + g, 1)], min_val=0, max_val=z.NP)
                        dve.wait_ge(part_turned[g], i + 1)
                        if g == 0:
                            at_least(dve, added[1], 2 * i)
                        else:
                            dve.wait_ge(added[0], 2 * i + 2)
                        add_window(g, at, added[g])

                    def step(i, first, last):
                        messages(i, 0)
                        messages(i, 1)
                        if not first:
                            add(i - 1, 1)
                        if not last:
                            onehots(i + 1, 0)
                        messages(i, 3)
                        messages(i, 2)
                        add(i, 0)
                        if not last:
                            onehots(i + 1, 1)

                    onehots(0, 0)
                    onehots(0, 1)
                    over_steps(dve, step)
                    add(L, 1)

                def general():
                    def group(g):
                        dve.wait_ge(g_in, 32 * g + 32)
                        nc.vector.tensor_copy(place_g[:, :], dst_g[:, :]).then_inc(g_place, 1)
                        nc.vector.tensor_copy(idx_g[:, 0:GRP], t["src16"][:, ds(g * GRP, GRP)])
                        nc.vector.tensor_copy(idx_g[:, GRP:2 * GRP], typ_g[:, :]).then_inc(g_set, 1)
                        dve.wait_ge(g_rows, (g + 1) * (2 * GRP * 16))
                        nc.vector.tensor_tensor(msg[:, :, 0:z.DX], hrow[:, 0:GRP, :], hrow[:, GRP:2 * GRP, :],
                                                ALU.mult).then_inc(g_msg, 1)
                        dve.wait_ge(g_msg, g + 1)
                        hold(dve, passed[2])

                        with dve.Fori(0, z.NT) as w:
                            u = g * z.NT + w
                            dve.wait_ge(g_place, g * (z.NT + 1) + w + 1)
                            for k in range(GRP):
                                nc.vector.tensor_scalar(member[:, k, :], t["iota"][:, :], place_g[:, k:k + 1], None,
                                                        ALU.is_equal).then_inc(g_member, 1) if k == GRP - 1 else \
                                    nc.vector.tensor_scalar(member[:, k, :], t["iota"][:, :], place_g[:, k:k + 1], None,
                                                            ALU.is_equal)
                            dve.wait_ge(g_member, u + 1)
                            nc.vector.tensor_scalar(place_g[:, :], place_g[:, :], -float(WIN), None,
                                                    ALU.add).then_inc(g_place, 1)
                            dve.wait_ge(g_turned, u + 1)
                            add_window(0, w * WIN, g_added)
                            dve.wait_ge(g_added, 2 * u + 2)
                            hold(dve, passed[2])

                    with dve.Fori(0, z.NG) as g:
                        group(g)

                fast_or_general(dve, fast, general)


def stage_5(nc, z, dram, t, out):
    ctx = ExitStack()
    with ctx:
        def sb(name, shape, dt):
            return ctx.enter_context(nc.sbuf_tensor(name, shape, dt))

        def sem(name):
            return ctx.enter_context(nc.semaphore(name))

        a_tile = sb("a_tile", [P, 2, 2, P], F32)
        b_tile = sb("b_tile", [2, 2, P], F32)
        row = sb("row", [P, 2, D], F32)
        done_row = sb("done_row", [P, 2, D], F32)
        deg = sb("in_deg", [P, 2, 1], F32)
        root = sb("in_root", [P, 2, 1], F32)
        norm = sb("in_norm", [P, 2, 1], F32)
        ps = [ctx.enter_context(nc.psum_tensor(f"ps_final{n}", [P, 512], F32)) for n in range(2)]
        row_in = [sem(f"row_in{s}") for s in range(2)]
        tile_ready = [sem(f"tile_ready{s}") for s in range(2)]
        product = [sem(f"product{s}") for s in range(2)]
        deg_ready = [sem(f"in_deg_ready{s}") for s in range(2)]
        root_ready = [sem(f"in_root_ready{s}") for s in range(2)]
        norm_ready = [sem(f"in_norm_ready{s}") for s in range(2)]
        row_done = [sem(f"row_done{s}") for s in range(2)]
        row_out = [sem(f"final_stored{s}") for s in range(2)]
        L = z.NT // 2 - 1

        def over_steps(eng, step):
            step(0)
            with eng.Fori(1, L) as i:
                step(i)
            step(L)

        with nc.Block() as block:
            @block.sync
            def _(sp):
                def load(i, s):
                    at_least(sp, row_done[s], i)
                    sp.dma_start(row[:, s, :], dram["base_out"][ds((i * 2 + s) * P, P), :]).then_inc(row_in[s], 16)

                def step(i):
                    for s in range(2):
                        load(i, s)
                over_steps(sp, step)

            @block.gpsimd
            def _(pool):
                def store(i, s, rows):
                    pool.wait_ge(row_done[s], i + 1)
                    pool.dma_start(out[ds((i * 2 + s) * P, rows), :], done_row[0:rows, s, :]).then_inc(row_out[s], 16)

                with pool.Fori(0, L) as i:
                    for s in range(2):
                        store(i, s, P)
                store(L, 0, P)
                store(L, 1, z.LAST)
                for s in range(2):
                    pool.wait_ge(row_out[s], 16 * (L + 1))

            @block.scalar
            def _(act):
                def take(i, s):
                    at_least(act, product[s], i)
                    tile = i * 2 + s
                    nc.scalar.copy(a_tile[:, s, :, :], t["acc"][:, :, ds(tile * P, P)])
                    nc.scalar.copy(b_tile[:, s, :], t["acc_ext"][:, ds(tile * P, P)]).then_inc(tile_ready[s], 1)

                def square_root(i, s):
                    act.wait_ge(deg_ready[s], i + 1)
                    at_least(act, norm_ready[s], i)
                    nc.scalar.activation(root[:, s, :], deg[:, s, :], ACT.Sqrt).then_inc(root_ready[s], 1)

                def step(i):
                    for s in range(2):
                        take(i, s)
                    for s in range(2):
                        square_root(i, s)
                over_steps(act, step)

            @block.tensor
            def _(pe):
                def step(i):
                    for s in range(2):
                        pe.wait_ge(tile_ready[s], i + 1)
                        at_least(pe, row_done[s], i)
                        for a in range(2):
                            nc.tensor.matmul(ps[s][:, 0:D], a_tile[:, s, a, :], t["w_agg"][:, a, :], start=(a == 0), stop=False)
                        nc.tensor.matmul(ps[s][:, 0:D], b_tile[:, s, :], t["w_ext"][:, 0:D], start=False, stop=True)
                        nc.tensor.matmul(ps[s][:, D:D + 1], b_tile[:, s, :], t["w_ext"][:, D:D + 1],
                                         start=True, stop=True).then_inc(product[s], 1)
                over_steps(pe, step)

            @block.vector
            def _(dve):
                def step(i):
                    for s in range(2):
                        dve.wait_ge(product[s], i + 1)
                        at_least(dve, root_ready[s], i)
                        nc.vector.tensor_scalar(deg[:, s, :], ps[s][:, D:D + 1], 1.0, None, ALU.max).then_inc(deg_ready[s], 1)
                    for s in range(2):
                        dve.wait_ge(root_ready[s], i + 1)
                        at_least(dve, row_done[s], i)
                        nc.vector.reciprocal(norm[:, s, :], root[:, s, :]).then_inc(norm_ready[s], 1)
                    for s in range(2):
                        dve.wait_ge(norm_ready[s], i + 1)
                        dve.wait_ge(row_in[s], 16 * i + 16)
                        at_least(dve, row_out[s], 16 * i)
                        nc.vector.scalar_tensor_tensor(out=done_row[:, s, :], in0=ps[s][:, 0:D], scalar=norm[:, s, :],
                                                       in1=row[:, s, :], op0=ALU.mult, op1=ALU.add).then_inc(row_done[s], 1)
                over_steps(dve, step)


def gnn_layer(nc, io, out):
    z = Sizes(io["x"].shape[0], io["src"].shape[0], io["rel"].shape[0])
    dram = {
        "h_tab": nc.dram_tensor("h_tab", [z.NP, z.DX], F32).ap(),
        "rg_tab": nc.dram_tensor("rg_tab", [z.R, z.DX], F32).ap(),
        "base_out": nc.dram_tensor("base_out", [z.NP, D], F32).ap(),
        "typ_row": nc.dram_tensor("typ_row", [z.NB * P * P], F16).ap(),
        "typ_cols": nc.dram_tensor("typ_cols", [P, z.CH], I16).ap(),
        "dst_cols": nc.dram_tensor("dst_cols", [P, z.CH], I16).ap(),
    }
    with ExitStack() as keep:
        t = {}

        def sb(ctx, name, shape, dt):
            t[name] = ctx.enter_context(nc.sbuf_tensor(name, shape, dt))

        sb(keep, "acc", [P, 2, z.ACCW], F32)
        t["x_all"] = t["acc"][:, :, :].rearrange("p a n -> p (a n)")[:, 0:z.NT * D].rearrange("p (t d) -> p t d", d=D)
        sb(keep, "ident", [P, P], F32)
        sb(keep, "iota", [P, P], F32)
        sb(keep, "ones", [P, P], F32)
        sb(keep, "eps", [P, 1], F32)
        sb(keep, "rel_id", [P, z.KT], F32)
        sb(keep, "src16", [P, z.CH], I16)
        sb(keep, "rel16", [P, z.CH], I16)
        sb(keep, "typ16", [P, z.STEPS, 2], I16)
        sb(keep, "table", [P, z.KT, 2, z.DM], F32R)
        sb(keep, "w_agg", [P, 2, D], F32)
        sb(keep, "w_ext", [2, z.DX], F32)
        sb(keep, "base_id", [1, z.NG], I32)
        sb(keep, "flag", [1, 1], I32)
        x_in = keep.enter_context(nc.semaphore("x_in"))
        with ExitStack() as early:
            sb(early, "iota_b", [P, P], BF16)
            sb(early, "src_lo", [P, z.CH], I32)
            sb(early, "src_hi", [P, z.CH], I32)
            sb(early, "upd_k", [P, 2, D], F32)
            sb(early, "upd_b", [1, D], F32)
            sb(early, "rstd", [P, z.NT], F32)
            sb(early, "shift", [P, z.NT], F32)
            sb(early, "src_norm", [P, z.NT], F32)
            stage_1(nc, z, io, dram, t, x_in)
            stage_2(nc, z, dram, t, x_in, None)
            stage_3(nc, z, dram, t)
        with ExitStack() as late:
            sb(late, "acc_ext", [2, z.ACCW], F32)
            stage_4(nc, z, dram, t)
            stage_5(nc, z, dram, t, out)


def kernel(x, src, dst, edge_type_500, L0_gnn_relation_emb, L0_gnn_msg_w, L0_gnn_msg_b, L0_gnn_upd_w, L0_gnn_upd_b,
           L0_gnn_gate_w, L0_gnn_gate_b):
    import numpy as np
    import concourse.bacc as bacc
    from concourse.bass_utils import run_bass_kernel_spmd

    laid_out = {
        "x": np.asarray(x),
        "src": np.asarray(src),
        "dst": np.asarray(dst),
        "typ": np.asarray(edge_type_500),
        "rel": np.asarray(L0_gnn_relation_emb),
        "msg_w": np.asarray(L0_gnn_msg_w).transpose(1, 0, 2),
        "msg_b": np.asarray(L0_gnn_msg_b).reshape(2, P).T,
        "upd_w": np.asarray(L0_gnn_upd_w).transpose(2, 1, 0),
        "upd_b": np.asarray(L0_gnn_upd_b).T.reshape(1, D),
        "gate_w": np.asarray(L0_gnn_gate_w).reshape(C, BL).T.reshape(1, D),
        "gate_b": np.asarray(L0_gnn_gate_b).reshape(1, 1),
    }
    nc = bacc.Bacc("TRN2", target_bir_lowering=False, num_devices=1)
    arrays, io = {}, {}
    for name, a in laid_out.items():
        arrays[f"in_{name}"] = np.ascontiguousarray(a)
        io[name] = nc.dram_tensor(f"in_{name}", a.shape, mybir.dt.from_np(a.dtype), kind="ExternalInput").ap()
    out = nc.dram_tensor("out", laid_out["x"].shape, F32, kind="ExternalOutput").ap()
    gnn_layer(nc, io, out)
    result = run_bass_kernel_spmd(nc, [arrays], core_ids=[0])
    return result.results[0]["out"]
```

```python
from contextlib import ExitStack

import concourse.bass as bass
from concourse import mybir

ALU = mybir.AluOpType
ACT = mybir.ActivationFunctionType
AX = mybir.AxisListType
F32 = mybir.dt.float32
F32R = mybir.dt.float32r
F16 = mybir.dt.float16
BF16 = mybir.dt.bfloat16
I32 = mybir.dt.int32
I16 = mybir.dt.int16
ds = bass.ds

P = 128
D = 256
C = 64
BL = 4
EPS = 1e-5
GRP = 4
BODY = 8
COUNT = 16
WIN = 128
PAD_ID = 16383
BLADE = [[0, 1, 2, 3], [1, 0, 3, 2], [2, 3, 0, 1], [3, 2, 1, 0]]
SIGN = [[1, 1, 1, -1], [1, 1, -1, 1], [1, 1, 1, -1], [1, 1, 1, 1]]


def at_least(eng, sem, value):
    if isinstance(value, int) and value <= 0:
        return
    eng.wait_ge(sem, value)


def hold(eng, passed):
    eng.sem_inc(passed, 1)


class Sizes:

    def __init__(self, n, e, r):
        self.N, self.E, self.R = n, e, r
        self.NT = -(-n // P)
        self.LAST = n - (self.NT - 1) * P
        self.NP = self.NT * P
        self.STEPS = -(-e // (P * BODY))
        self.CH = self.STEPS * BODY
        self.NG = self.CH // GRP
        self.NB = -(-self.CH // P)
        self.CB = self.CH - (self.NB - 1) * P
        self.FULL = e // P - (self.NB - 1) * P
        self.REST = e % P
        self.KT = -(-r // P)
        self.RL = r - (self.KT - 1) * P
        self.ACCW = self.NP + WIN
        self.DX = D + 1
        self.DM = D + 2
        self.PER = self.CH // self.NT
        assert self.NT % 14 == 0 and self.NP <= 16000 and r <= 2048
        assert self.PER * self.NT == self.CH and self.PER == COUNT and 0 < self.FULL < P and self.KT > 1


def stage_1(nc, z, io, dram, t, x_in):
    ctx = ExitStack()
    with ctx:
        def sb(name, shape, dt):
            return ctx.enter_context(nc.sbuf_tensor(name, shape, dt))

        def sem(name):
            return t["sems"].enter_context(nc.semaphore(name))

        lists = ["src", "dst", "typ"]
        rows_i = [sb(f"rows_i_{n}", [P, z.NB, P], I32) for n in lists]
        rows_f = [r[:, :, :].bitcast(F32) for r in rows_i]
        rows_h = sb("rows_h", [P, z.NB, P], F16)
        cols = [sb(f"cols_{n}", [P, z.CH], F32) for n in lists]
        base = sb("base", [P, z.NG], F32)
        whole, digit = (rows_i[0][:, :, :].rearrange("p b j -> p (b j)")[:, 0:z.CH],
                        rows_i[1][:, :, :].rearrange("p b j -> p (b j)")[:, 0:z.CH])
        far, here = cols[0], cols[2]
        bad = sb("bad", [P, 1], F32)
        col16 = [sb(f"col16_{n}", [P, z.CH], I16) for n in ("dst", "typ")]
        upd_w = sb("upd_w", [P, C, BL], F32)
        msg_w = sb("msg_w", [P, BL, C], F32)
        msg_k = sb("msg_k", [P, 2, D], F32)
        msg_b = sb("msg_b", [P, 2], F32)
        upd_b = sb("upd_b", [2, D], F32)
        upd_b_high = sb("upd_b_high", [2, D], F32R)
        rel = sb("rel", [P, z.KT, D], F32)
        gate_w = sb("gate_w", [P, D], F32)
        gate_b = sb("gate_b", [P, 1], F32)
        logit = sb("logit", [P, z.KT], F32)
        gate = sb("gate", [P, z.KT], F32)
        gated = sb("gated", [P, z.KT, z.DM], F32)
        prod = gated
        pt = [ctx.enter_context(nc.psum_tensor(f"turn{n}", [P, 512], F32)) for n in range(8)]

        pads_set = sem("pads_set")
        consts_set = sem("consts_set")
        iotas_set = sem("iotas_set")
        list_in = [sem(f"in_{n}") for n in lists]
        cast = sem("lists_cast")
        half_cast = sem("typ_half_cast")
        turned = sem("turned")
        unloaded = sem("turn_unloaded")
        cols_ready = sem("cols_ready")
        base_ps = sem("base_in_psum")
        chain = sem("vector_chain")
        bad_ready = sem("bad_ready")
        bad_ps = sem("bad_in_psum")
        w_in = sem("weights_in")
        w_built = sem("weights_built")
        w_ps = sem("weights_in_psum")
        rel_zero = sem("rel_zeroed")
        rel_in = sem("rel_in")
        logit_ready = sem("logit_ready")
        gate_ready = sem("gate_ready")
        gated_ready = sem("gated_ready")
        stored = sem("stage1_stored")
        x_zero = sem("x_zeroed")

        banks = [list(range(b, min(b + 4, z.NB))) for b in range(0, z.NB, 4)]
        assert len(banks) == 4

        with nc.Block() as block:
            @block.sync
            def _(sp):
                sp.wait_ge(pads_set, 3)
                for n, arr in enumerate((io["src"], io["dst"], io["typ"])):
                    full = (z.NB - 1) * P * P
                    sp.dma_start(rows_i[n][:, 0:z.NB - 1, :],
                                 arr[0:full].rearrange("(b p j) -> p b j", p=P, j=P)).then_inc(list_in[n], 16)
                    sp.dma_start(rows_i[n][0:z.FULL, z.NB - 1, :],
                                 arr[full:full + z.FULL * P].rearrange("(p j) -> p j", j=P)).then_inc(list_in[n], 16)
                    sp.dma_start(rows_i[n][z.FULL:z.FULL + 1, z.NB - 1, 0:z.REST],
                                 arr[z.E - z.REST:z.E].rearrange("(p j) -> p j", p=1)).then_inc(list_in[n], 16)
                for h in range(2):
                    sp.dma_start(upd_w[C * h:C * h + C, :, :], io["upd_w"]).then_inc(w_in, 16)
                    sp.dma_start(msg_w[C * h:C * h + C, :, :], io["msg_w"]).then_inc(w_in, 16)
                sp.dma_start(msg_b[:, :], io["msg_b"]).then_inc(w_in, 16)
                sp.dma_start(upd_b[:, :], io["upd_b"].to_broadcast((2, D))).then_inc(w_in, 16)
                sp.wait_ge(rel_zero, 1)
                sp.dma_start(rel[:, 0:z.KT - 1, :],
                             io["rel"][0:(z.KT - 1) * P, :].rearrange("(k p) d -> p k d", p=P)).then_inc(rel_in, 16)
                sp.dma_start(rel[0:z.RL, z.KT - 1, :], io["rel"][(z.KT - 1) * P:z.R, :]).then_inc(rel_in, 16)
                sp.dma_start(gate_w[:, :], io["gate_w"].to_broadcast((P, D))).then_inc(rel_in, 16)
                sp.dma_start(gate_b[:, :], io["gate_b"].to_broadcast((P, 1))).then_inc(rel_in, 16)
                sp.wait_ge(x_zero, 1)
                for c in range(0, z.NT - 14, 14):
                    sp.dma_start(t["x_all"][:, c:c + 14, :],
                                 io["x"][c * P:(c + 14) * P, :].rearrange("(t p) d -> p t d", p=P)).then_inc(x_in, 16)
                c = z.NT - 14
                sp.dma_start(t["x_all"][:, c:c + 13, :],
                             io["x"][c * P:(c + 13) * P, :].rearrange("(t p) d -> p t d", p=P)).then_inc(x_in, 16)
                sp.dma_start(t["x_all"][0:z.LAST, z.NT - 1, :], io["x"][z.NP - P:z.N, :]).then_inc(x_in, 16)

            @block.scalar
            def _(act):
                act.wait_ge(w_in, 96)
                upd_cols = t["upd_k"][:, :, :].rearrange("p h (c b) -> p h c b", b=BL)
                for i in range(BL):
                    for j in range(BL):
                        p0 = C * (j % 2)
                        nc.scalar.mul(upd_cols[p0:p0 + C, j // 2, :, i], upd_w[p0:p0 + C, :, BLADE[i][j]],
                                      float(SIGN[i][j])).then_inc(w_built, 1)
                        p0 = C * (i % 2)
                        nc.scalar.mul(msg_k[p0:p0 + C, i // 2, C * j:C * j + C], msg_w[p0:p0 + C, BLADE[i][j], :],
                                      float(SIGN[i][j])).then_inc(w_built, 1)
                act.wait_ge(logit_ready, 1)
                nc.scalar.activation(gate[:, :], logit[:, :], ACT.Sigmoid, bias=gate_b[:, :]).then_inc(gate_ready, 1)
                act.wait_ge(half_cast, 1)
                act.dma_start(dram["typ_row"].rearrange("(b p j) -> p b j", p=P, j=P), rows_h[:, :, :]).then_inc(stored, 16)
                act.wait_ge(cols_ready, 2)
                act.dma_start(dram["dst_cols"], col16[0][:, :]).then_inc(stored, 16)
                act.dma_start(dram["typ_cols"], col16[1][:, :]).then_inc(stored, 16)
                act.wait_ge(gated_ready, 2 * z.KT + 1)
                act.dma_start(dram["rg_tab"][0:(z.KT - 1) * P, :].rearrange("(k p) d -> p k d", p=P),
                              gated[:, 0:z.KT - 1, 0:z.DX]).then_inc(stored, 16)
                act.dma_start(dram["rg_tab"][(z.KT - 1) * P:z.R, :],
                              gated[0:z.RL, z.KT - 1, 0:z.DX]).then_inc(stored, 16)
                act.wait_ge(stored, 80)

            @block.gpsimd
            def _(pool):
                for n in range(3):
                    nc.gpsimd.memset(rows_i[n][:, z.NB - 1, :], PAD_ID).then_inc(pads_set, 1)
                nc.gpsimd.memset(rel[:, z.KT - 1, :], 0.0).then_inc(rel_zero, 1)
                nc.gpsimd.memset(t["x_all"][:, z.NT - 1, :], 0.0).then_inc(x_zero, 1)
                nc.gpsimd.memset(t["ident"][:, :], 0.0).then_inc(consts_set, 1)
                nc.gpsimd.memset(t["ones"][:, :], 1.0).then_inc(consts_set, 1)
                nc.gpsimd.memset(t["minus_ones"][:, :].bitcast(F32), -1.0).then_inc(consts_set, 1)
                nc.gpsimd.memset(t["eps"][:, :], EPS).then_inc(consts_set, 1)
                pool.wait_ge(consts_set, 1)
                nc.gpsimd.affine_select(out=t["ident"][:, :], in_=t["ident"][:, :], compare_op=ALU.not_equal, fill=1.0,
                                        base=0, pattern=[[-1, P]], channel_multiplier=1).then_inc(iotas_set, 1)
                nc.gpsimd.iota(t["iota"][:, :], [[1, P]], base=0, channel_multiplier=0,
                               allow_small_or_imprecise_dtypes=True).then_inc(iotas_set, 1)
                nc.gpsimd.iota(t["iota_k"][:, :, :], [[1, P], [0, COUNT]], base=0, channel_multiplier=0,
                               allow_small_or_imprecise_dtypes=True).then_inc(iotas_set, 1)
                nc.gpsimd.iota(t["rel_id"][:, :], [[P, z.KT]], base=0, channel_multiplier=1,
                               allow_small_or_imprecise_dtypes=True).then_inc(iotas_set, 1)

            @block.tensor
            def _(pe):
                pe.wait_ge(iotas_set, 1)
                pe.wait_ge(consts_set, 2)
                for n in range(3):
                    pe.wait_ge(cast, n + 1)
                    for b, blocks in enumerate(banks):
                        if n == 2:
                            pe.wait_ge(unloaded, b + 1)
                        for k, blk in enumerate(blocks):
                            rows = P if blk < z.NB - 1 else z.CB
                            mm = nc.tensor.transpose(pt[4 * (n % 2) + b][:, k * P:k * P + rows],
                                                     rows_f[n][0:rows, blk, :], t["ident"][0:rows, 0:rows])
                        mm.then_inc(turned, 1)
                pe.wait_ge(unloaded, 8)
                nc.tensor.matmul(pt[4][:, 0:z.NG], t["ones"][0:1, :], cols[1][0:1, 0:z.CH:GRP],
                                 start=True, stop=True).then_inc(base_ps, 1)
                pe.wait_ge(w_built, 2 * BL * BL)
                for i in range(2):
                    for m in range(2):
                        nc.tensor.matmul(pt[5][:, i * D:i * D + D], msg_k[:, m, i * P:i * P + P], t["upd_k"][:, m, :],
                                         start=(m == 0), stop=(m == 1))
                for m in range(2):
                    mm = nc.tensor.matmul(pt[6][0:1, 0:D], msg_b[:, m:m + 1], t["upd_k"][:, m, :],
                                          start=(m == 0), stop=(m == 1))
                mm.then_inc(w_ps, 1)
                pe.wait_ge(bad_ready, 1)
                nc.tensor.matmul(pt[7][0:1, 0:1], bad[:, :], t["ones"][:, 0:1], start=True, stop=True).then_inc(bad_ps, 1)

            @block.vector
            def _(dve):
                links = [0]

                def link(ins):
                    links[0] += 1
                    ins.then_inc(chain, 1)
                    dve.wait_ge(chain, links[0])

                for n in range(3):
                    dve.wait_ge(list_in[n], 48)
                    nc.vector.tensor_copy(rows_f[n], rows_i[n][:, :, :]).then_inc(cast, 1)
                dve.wait_ge(cast, 3)
                nc.vector.tensor_copy(rows_h[:, :, :], rows_f[2]).then_inc(half_cast, 1)
                dve.wait_ge(rel_in, 64)
                for k in range(z.KT):
                    nc.vector.tensor_tensor(prod[:, k, 0:D], rel[:, k, :], gate_w[:, :], ALU.mult).then_inc(chain, 1)
                links[0] += z.KT
                dve.wait_ge(chain, links[0])
                nc.vector.tensor_reduce(logit[:, :], prod[:, :, 0:D], AX.X, ALU.add).then_inc(logit_ready, 1)

                def unload(n):
                    for b, blocks in enumerate(banks):
                        dve.wait_ge(turned, 4 * n + b + 1)
                        width = min(4 * P, z.CH - b * 4 * P)
                        nc.vector.tensor_copy(cols[n][:, b * 4 * P:b * 4 * P + width],
                                              pt[4 * (n % 2) + b][:, 0:width]).then_inc(unloaded, 1)

                unload(0)
                dve.wait_ge(unloaded, 4)
                dve.wait_ge(turned, 8)
                nc.vector.tensor_scalar(t["src16"][:, :], cols[0][:, :], float(z.N - 1), None, ALU.min).then_inc(chain, 1)
                links[0] += 1
                link(nc.vector.tensor_copy(whole[:, :], cols[0][:, :]))
                link(nc.vector.tensor_scalar(digit[:, :], whole[:, :], P - 1, None, ALU.bitwise_and))
                link(nc.vector.tensor_copy(t["src_lo"][:, :], digit[:, :]))
                link(nc.vector.tensor_scalar(digit[:, :], whole[:, :], 7, None, ALU.arith_shift_right))
                link(nc.vector.tensor_copy(t["src_hi"][:, :], digit[:, :]))
                unload(1)
                unload(2)
                dve.wait_ge(unloaded, 12)
                nc.vector.tensor_copy(col16[0][:, :], cols[1][:, :]).then_inc(cols_ready, 1)
                nc.vector.tensor_scalar(col16[1][:, :], cols[2][:, :], float(z.R - 1), None, ALU.min).then_inc(cols_ready, 1)
                dve.wait_ge(cols_ready, 2)
                dve.wait_ge(base_ps, 1)
                link(nc.vector.tensor_scalar(base[:, :], pt[4][:, 0:z.NG], float(z.NP), 0.0, ALU.min, ALU.max))
                nc.vector.tensor_copy(t["base_id"][:, :], base[0:1, :]).then_inc(chain, 1)
                links[0] += 1
                link(nc.vector.tensor_tensor(far[:, :].rearrange("p (g k) -> p g k", k=GRP),
                                             cols[1][:, :].rearrange("p (g k) -> p g k", k=GRP),
                                             base[:, :].to_broadcast((P, z.NG, GRP)), ALU.subtract))
                link(nc.vector.tensor_scalar(here[:, :], cols[1][:, :], float(PAD_ID), None, ALU.is_lt))
                link(nc.vector.tensor_scalar(t["minus_place"][:, :], far[:, :], 2000.0, -1.0, ALU.min, ALU.mult))
                nc.vector.tensor_scalar(cols[1][:, :], far[:, :], 0.0, None, ALU.is_lt).then_inc(chain, 1)
                links[0] += 1
                link(nc.vector.tensor_scalar(far[:, :], far[:, :], float(WIN), None, ALU.is_ge))
                link(nc.vector.tensor_tensor(far[:, :], far[:, :], here[:, :], ALU.mult))
                link(nc.vector.tensor_tensor(far[:, :], far[:, :], cols[1][:, :], ALU.add))
                nc.vector.tensor_reduce(bad[:, :], far[:, :], AX.X, ALU.add).then_inc(bad_ready, 1)
                dve.wait_ge(gate_ready, 1)
                for k in range(z.KT):
                    nc.vector.tensor_scalar(gated[:, k, 0:D], rel[:, k, :], gate[:, k:k + 1], None,
                                            ALU.mult).then_inc(gated_ready, 1)
                    nc.vector.tensor_copy(gated[:, k, D:D + 1], gate[:, k:k + 1]).then_inc(gated_ready, 1)
                nc.vector.memset(gated[:, :, D + 1:D + 2], 0.0).then_inc(gated_ready, 1)
                dve.wait_ge(gated_ready, 2 * z.KT + 1)
                link(nc.vector.tensor_copy(t["table"][:, :, 0, :], gated[:, :, :]))
                link(nc.vector.tensor_tensor(t["table"][:, :, 1, :], gated[:, :, :],
                                             t["table"][:, :, 0, :].bitcast(F32), ALU.subtract))
                dve.wait_ge(iotas_set, 4)
                dve.wait_ge(w_in, 96)
                link(nc.vector.tensor_copy(upd_b_high[:, :], upd_b[:, :]))
                link(nc.vector.scalar_tensor_tensor(out=t["upd_b2"][:, :], in0=upd_b_high[:, :].bitcast(F32),
                                                    scalar=t["rel_id"][0:2, 0:1], in1=upd_b[:, :],
                                                    op0=ALU.mult, op1=ALU.subtract))
                dve.wait_ge(w_ps, 1)
                link(nc.vector.tensor_copy(t["w_agg"][:, :, :], pt[5][:, :].rearrange("p (h d) -> p h d", h=2)))
                link(nc.vector.tensor_copy(t["w_ext"][:, :], pt[6][0:1, 0:D]))
                dve.wait_ge(bad_ps, 1)
                link(nc.vector.tensor_copy(t["flag"][:, :], pt[7][0:1, 0:1]))


def stage_2(nc, z, dram, t, x_in):
    ctx = ExitStack()
    with ctx:
        def sb(name, shape, dt):
            return ctx.enter_context(nc.sbuf_tensor(name, shape, dt))

        def sem(name):
            return t["sems"].enter_context(nc.semaphore(name))

        SLOT = COUNT
        SLOTS = 2 * z.PER // SLOT
        HI = z.NT
        one_lo = sb("one_lo", [P, SLOTS, P, SLOT], BF16)
        one_hi = sb("one_hi", [P, SLOTS, HI, SLOT], BF16)
        zero_b = sb("zero_b", [P, P], BF16)
        stats = sb("stats", [P, z.NT, 6], F32)
        mean = sb("mean", [P, z.NT], F32)
        half = sb("half", [P, z.NT], F32)
        var = sb("var", [P, z.NT], F32)
        std = sb("std", [P, z.NT], F32)
        h = sb("h", [P, 2, D], F32)
        h_t = sb("h_t", [P, 2, D], F32)
        base_row = sb("base_row", [P, 2, D], F32)
        deg = sb("deg", [P, z.NT], F32)
        ps_turn = [ctx.enter_context(nc.psum_tensor(f"ps_turn{n}", [P, 512], F32)) for n in range(2)]
        ps_out = [ctx.enter_context(nc.psum_tensor(f"ps_out{n}", [P, 512], F32)) for n in range(2)]
        ps_deg = ctx.enter_context(nc.psum_tensor("ps_deg", [P, 512], F32))

        stats_ready = sem("stats_ready")
        moments = sem("moments")
        var_ready = sem("var_ready")
        std_ready = sem("std_ready")
        norm_ready = sem("norm_ready")
        onehots = sem("onehots_ready")
        counted = sem("onehots_counted")
        h_ready = [sem(f"h_ready{n}") for n in range(2)]
        turned = [sem(f"h_turned{n}") for n in range(2)]
        t_ready = [sem(f"h_t_ready{n}") for n in range(2)]
        summed = [sem(f"row_summed{n}") for n in range(2)]
        row_ready = [sem(f"row_ready{n}") for n in range(2)]
        x_added = [sem(f"x_added{n}") for n in range(2)]
        row_out = [sem(f"row_stored{n}") for n in range(2)]
        zeros = sem("zeros_ready")
        deg_done = sem("deg_done")
        deg_ready = sem("deg_clamped")
        root_ready = sem("deg_root_ready")
        link2 = sem("stage2_chain")
        passed = sem("stage2_sp_passed")
        STEP = 2
        N_STEPS = z.NT // STEP

        with nc.Block() as block:
            @block.gpsimd
            def _(pool):
                with pool.Fori(0, N_STEPS) as i:
                    for s in range(STEP):
                        pool.wait_ge(row_ready[s], i + 1)
                        row = base_row[:, s:s + 1, :]
                        nc.gpsimd.tensor_tensor(row, row, t["x_all"][:, ds(i * STEP + s, 1), :], ALU.add).then_inc(x_added[s], 1)

            @block.sync
            def _(sp):
                def step(i):
                    for s in range(STEP):
                        sp.wait_ge(x_added[s], i + 1)
                        hold(sp, passed)
                        sp.dma_start(dram["base_out"][ds((i * STEP + s) * P, P), :], base_row[:, s, :]).then_inc(row_out[s], 16)

                with sp.Fori(0, N_STEPS) as i:
                    step(i)
                for s in range(STEP):
                    sp.wait_ge(row_out[s], 16 * N_STEPS)

            @block.scalar
            def _(act):
                act.wait_ge(var_ready, 1)
                nc.scalar.activation(std[:, :], var[:, :], ACT.Sqrt, bias=t["eps"][:, :]).then_inc(std_ready, 1)
                act.wait_ge(norm_ready, 2)

                def step(i):
                    for s in range(STEP):
                        tile = i * STEP + s
                        at_least(act, turned[s], i)
                        nc.scalar.activation(h[:, s, :].rearrange("p (a d) -> p a d", a=1), t["x_all"][:, ds(tile, 1), :],
                                             ACT.Relu, bias=t["shift"][:, ds(tile, 1)],
                                             scale=t["rstd"][:, ds(tile, 1)]).then_inc(h_ready[s], 1)
                    for s in range(STEP):
                        act.wait_ge(turned[s], i + 1)
                        at_least(act, summed[s], i)
                        nc.scalar.copy(h_t[:, s, :], ps_turn[s][:, 0:D]).then_inc(t_ready[s], 1)
                    for s in range(STEP):
                        act.wait_ge(summed[s], i + 1)
                        at_least(act, row_out[s], 16 * i)
                        nc.scalar.copy(base_row[:, s, :], ps_out[s][:, 0:D]).then_inc(row_ready[s], 1)

                step(0)
                with act.Fori(1, N_STEPS) as i:
                    step(i)
                act.wait_ge(deg_ready, 1)
                nc.scalar.activation(deg[:, :], deg[:, :], ACT.Sqrt).then_inc(root_ready, 1)

            @block.tensor
            def _(pe):
                pe.wait_ge(zeros, 1)
                nc.tensor.matmul(ps_deg[:, 0:HI], zero_b[:, :], zero_b[:, 0:HI], start=True, stop=False)

                def count(n, b):
                    pe.wait_ge(onehots, n + 1)
                    for k in range(SLOT):
                        mm = nc.tensor.matmul(ps_deg[:, 0:HI], one_lo[:, b, :, k], one_hi[:, b, :, k],
                                              start=False, stop=False)
                    mm.then_inc(counted, 1)

                def step(i):
                    for s in range(STEP):
                        pe.wait_ge(h_ready[s], i + 1)
                        at_least(pe, t_ready[s], i)
                        for a in range(2):
                            mm = nc.tensor.transpose(ps_turn[s][:, a * P:a * P + P], h[:, s, a * P:a * P + P], t["ident"][:, :])
                        mm.then_inc(turned[s], 1)
                    for s in range(STEP):
                        pe.wait_ge(t_ready[s], i + 1)
                        at_least(pe, row_ready[s], i)
                        nc.tensor.matmul(ps_out[s][:, 0:D], t["minus_ones"][:, :], t["upd_b2"][:, :], start=True, stop=False)
                        for a in range(2):
                            mm = nc.tensor.matmul(ps_out[s][:, 0:D], h_t[:, s, a * P:a * P + P], t["upd_k"][:, a, :],
                                                  start=False, stop=(a == 1))
                        mm.then_inc(summed[s], 1)
                        count(i * SLOTS + s, s)

                step(0)
                with pe.Fori(1, N_STEPS) as i:
                    step(i)
                nc.tensor.matmul(ps_deg[:, 0:HI], zero_b[:, :], zero_b[:, 0:HI], start=False, stop=True).then_inc(deg_done, 1)

            @block.vector
            def _(dve):
                nc.vector.memset(zero_b[:, :], 0.0).then_inc(zeros, 1)
                dve.wait_ge(x_in, 16 * (z.NT // 14 + 1))
                with dve.Fori(0, z.NT // 14) as i:
                    for k in range(14):
                        tile = ds(i * 14 + k, 1)
                        nc.vector.bn_stats(stats[:, tile, :].rearrange("p a c -> p (a c)"),
                                           t["x_all"][:, tile, :].rearrange("p a d -> p (a d)")).then_inc(stats_ready, 1)
                dve.wait_ge(stats_ready, z.NT)
                nc.vector.tensor_tensor(mean[:, :], stats[:, :, 1], stats[:, :, 4], ALU.add).then_inc(moments, 1)
                nc.vector.tensor_tensor(half[:, :], stats[:, :, 1], stats[:, :, 4], ALU.subtract).then_inc(moments, 1)
                nc.vector.tensor_tensor(var[:, :], stats[:, :, 2], stats[:, :, 5], ALU.add).then_inc(moments, 1)
                dve.wait_ge(moments, 2)
                nc.vector.scalar_tensor_tensor(out=half[:, :], in0=half[:, :], scalar=0.25, in1=half[:, :],
                                               op0=ALU.mult, op1=ALU.mult).then_inc(moments, 1)
                dve.wait_ge(moments, 4)
                nc.vector.scalar_tensor_tensor(out=var[:, :], in0=var[:, :], scalar=1.0 / D, in1=half[:, :],
                                               op0=ALU.mult, op1=ALU.add).then_inc(var_ready, 1)
                dve.wait_ge(std_ready, 1)
                nc.vector.reciprocal(t["rstd"][:, :], std[:, :]).then_inc(norm_ready, 1)
                dve.wait_ge(norm_ready, 1)
                nc.vector.scalar_tensor_tensor(out=t["shift"][:, :], in0=mean[:, :], scalar=-0.5, in1=t["rstd"][:, :],
                                               op0=ALU.mult, op1=ALU.mult).then_inc(norm_ready, 1)

                def step(i):
                    for b in range(SLOTS):
                        at_least(dve, counted, i * SLOTS + b + 1 - SLOTS)
                        chunks = ds((i * SLOTS + b) * SLOT, SLOT)
                        nc.vector.tensor_tensor(one_lo[:, b, :, :], t["iota_k"][:, :, :],
                                                t["src_lo"][:, chunks].rearrange("p (a k) -> p a k", a=1).to_broadcast((P, P, SLOT)),
                                                ALU.is_equal)
                        last = nc.vector.tensor_tensor(one_hi[:, b, :, :], t["iota_k"][:, 0:HI, :],
                                                       t["src_hi"][:, chunks].rearrange("p (a k) -> p a k", a=1).to_broadcast((P, HI, SLOT)),
                                                       ALU.is_equal)
                        last.then_inc(onehots, 1)

                step(0)
                with dve.Fori(1, N_STEPS) as i:
                    step(i)
                dve.wait_ge(deg_done, 1)
                nc.vector.tensor_scalar(deg[:, :], ps_deg[:, 0:HI], 1.0, None, ALU.max).then_inc(deg_ready, 1)
                dve.wait_ge(root_ready, 1)
                nc.vector.reciprocal(t["src_norm"][:, :], deg[:, :]).then_inc(link2, 1)
                dve.wait_ge(link2, 1)
                nc.vector.tensor_tensor(t["rstd"][:, :], t["rstd"][:, :], t["src_norm"][:, :], ALU.mult).then_inc(link2, 1)
                nc.vector.tensor_tensor(t["shift"][:, :], t["shift"][:, :], t["src_norm"][:, :], ALU.mult).then_inc(link2, 1)


def stage_3(nc, z, dram, t):
    ctx = ExitStack()
    with ctx:
        def sem(name):
            return t["sems"].enter_context(nc.semaphore(name))

        LOT = 7
        BY_ACT = 5
        rows = [ctx.enter_context(nc.sbuf_tensor(f"hs_rows{s}", [P, LOT, z.DX], F32)) for s in range(2)]
        zeros = ctx.enter_context(nc.sbuf_tensor("zeros", [P, LOT, D], F32))
        act_done = [sem(f"hs_act{s}") for s in range(2)]
        dve_half = [sem(f"hs_scaled{s}") for s in range(2)]
        dve_done = [sem(f"hs_dve{s}") for s in range(2)]
        zeroed = sem("x_zeroed_again")
        passed = sem("stage3_sp_passed")
        out = [sem(f"hs_stored{s}") for s in range(2)]
        STEPS = z.NT // (2 * LOT)

        with nc.Block() as block:
            @block.sync
            def _(sp):
                with sp.Fori(0, STEPS) as i:
                    for s in range(2):
                        sp.wait_ge(act_done[s], (i + 1) * BY_ACT)
                        hold(sp, passed)
                        sp.wait_ge(dve_done[s], (i + 1) * 2)
                        hold(sp, passed)
                        sp.dma_start(dram["h_tab"][ds((i * 2 + s) * (LOT * P), LOT * P), :].rearrange("(t p) d -> p t d", p=P),
                                     rows[s][:, :, :]).then_inc(out[s], 16)
                for s in range(2):
                    sp.wait_ge(out[s], 16 * STEPS)

            @block.scalar
            def _(act):
                def step(i):
                    for s in range(2):
                        at_least(act, out[s], 16 * i)
                        for k in range(BY_ACT):
                            tile = (i * 2 + s) * LOT + k
                            nc.scalar.activation(rows[s][:, k:k + 1, 0:D], t["x_all"][:, ds(tile, 1), :],
                                                 ACT.Relu, bias=t["shift"][:, ds(tile, 1)],
                                                 scale=t["rstd"][:, ds(tile, 1)]).then_inc(act_done[s], 1)
                step(0)
                with act.Fori(1, STEPS) as i:
                    step(i)

            @block.vector
            def _(dve):
                def step(i):
                    for s in range(2):
                        at_least(dve, out[s], 16 * i)
                        for k in range(BY_ACT, LOT):
                            tile = (i * 2 + s) * LOT + k
                            nc.vector.tensor_scalar(rows[s][:, k:k + 1, 0:D], t["x_all"][:, ds(tile, 1), :],
                                                    t["rstd"][:, ds(tile, 1)], t["shift"][:, ds(tile, 1)],
                                                    ALU.mult, ALU.add).then_inc(dve_half[s], 1)
                        nc.vector.tensor_copy(rows[s][:, :, D], t["src_norm"][:, ds((i * 2 + s) * LOT, LOT)]).then_inc(dve_done[s], 1)
                        dve.wait_ge(dve_half[s], (i + 1) * (LOT - BY_ACT))
                        nc.vector.tensor_scalar(rows[s][:, BY_ACT:LOT, 0:D], rows[s][:, BY_ACT:LOT, 0:D], 0.0, None,
                                                ALU.max).then_inc(dve_done[s], 1)
                        dve.wait_ge(act_done[s], (i + 1) * BY_ACT)
                        nc.vector.tensor_copy(t["x_all"][:, ds((i * 2 + s) * LOT, LOT), :], zeros[:, :, :]).then_inc(zeroed, 1)
                nc.vector.memset(zeros[:, :, :], 0.0).then_inc(zeroed, 1)
                dve.wait_ge(zeroed, 1)
                step(0)
                with dve.Fori(1, STEPS) as i:
                    step(i)


def stage_4(nc, z, dram, t):
    ctx = ExitStack()
    with ctx:
        def sb(name, shape, dt):
            return ctx.enter_context(nc.sbuf_tensor(name, shape, dt))

        def sem(name):
            return t["sems"].enter_context(nc.semaphore(name))

        PAIRS = BODY // 2
        L = z.STEPS - 1
        hrow = sb("hrow", [P, BODY, z.DX], F32)
        high = sb("high", [P, 4, z.DM], F32R)
        low = sb("low", [P, 4, z.DM], F32R)
        off = sb("off", [P, 4, WIN], BF16)
        member = sb("member", [P, 4, WIN], F32R)
        typ_b = sb("typ_b", [P, 2, GRP * P], F16)
        one = sb("one", [P, 2, z.KT, GRP * P], F32R)
        part = sb("part", [P, 2, z.DM], F32)
        idx = sb("idx", [P, 2, GRP], I32)
        dst_g = sb("dst_g", [P, GRP], I16)
        typ_g = sb("typ_g", [P, GRP], I16)
        place_g = sb("place_g", [P, GRP], F32)
        idx_g = sb("idx_g", [P, 2 * GRP], I32)
        ps_rel = [ctx.enter_context(nc.psum_tensor(f"ps_rel{n}", [P, 2, 512], F32)) for n in range(2)]
        ps_sum = [ctx.enter_context(nc.psum_tensor(f"ps_sum{n}", [P, 512], F32)) for n in range(2)]
        ps_tr = [ctx.enter_context(nc.psum_tensor(f"ps_tr{n}", [P, 512], F32)) for n in range(2)]

        consts = sem("ends_set")
        zeroed = sem("acc_zeroed")
        idx_ready = [sem(f"idx_ready{g}") for g in range(2)]
        h_in = [sem(f"hrow_in{k}") for k in range(BODY)]
        typ_in = [sem(f"typ_in{g}") for g in range(2)]
        one_ready = [sem(f"one_ready{g}") for g in range(2)]
        rel_ready = [sem(f"rel_ready{q}") for q in range(PAIRS)]
        msg_ready = [sem(f"msg_ready{q}") for q in range(PAIRS)]
        high_ready = [sem(f"high_ready{q}") for q in range(PAIRS)]
        off_ready = sem("off_ready")
        low_ready = [sem(f"low_ready{q}") for q in range(PAIRS)]
        summed = [sem(f"summed{q}") for q in range(PAIRS)]
        part_ready = [sem(f"part_ready{g}") for g in range(2)]
        part_turned = [sem(f"part_turned{g}") for g in range(2)]
        added = [sem(f"added{g}") for g in range(2)]
        passed = [sem(f"passed_{n}") for n in ("pool", "sp", "dve")]
        g_in, g_set, g_rows, g_msg, g_high, g_low, g_place, g_member, g_sum, g_part, g_turned, g_added = (
            sem(n) for n in ("g_in", "g_set", "g_rows", "g_msg", "g_high", "g_low", "g_place", "g_member", "g_sum",
                             "g_part", "g_turned", "g_added"))

        def fast_or_general(eng, fast, general):
            outside = eng.value_load(t["flag"][0:1, 0:1], min_val=0, max_val=z.CH * P)
            with eng.If(outside == 0):
                fast()
            with eng.Else():
                general()

        def over_steps(eng, step):
            step(0, True, False)
            with eng.Fori(1, L) as i:
                step(i, False, False)
            step(L, False, True)

        def places(q):
            return slice(2 * (q % 2), 2 * (q % 2) + 2)

        def with_step(q, i):
            return q % PAIRS, i + 1 + q // PAIRS

        with nc.Block() as block:
            @block.sync
            def _(sp):
                def load(i, g):
                    at_least(sp, one_ready[g], i)
                    hold(sp, passed[1])
                    sp.dma_start(typ_b[:, g, :], dram["typ_row"][ds(i * (BODY * P) + g * GRP * P, GRP * P)].rearrange(
                        "(a n) -> a n", a=1).to_broadcast((P, GRP * P))).then_inc(typ_in[g], 16)

                def fast():
                    load(0, 0)
                    load(0, 1)
                    with sp.Fori(1, z.STEPS) as i:
                        load(i, 0)
                        load(i, 1)

                def general():
                    def group(g):
                        at_least(sp, g_set, g)
                        hold(sp, passed[1])
                        sp.dma_start(dst_g[:, :], dram["dst_cols"][:, ds(g * GRP, GRP)]).then_inc(g_in, 16)
                        sp.dma_start(typ_g[:, :], dram["typ_cols"][:, ds(g * GRP, GRP)]).then_inc(g_in, 16)
                    group(0)
                    with sp.Fori(1, z.NG) as g:
                        group(g)

                fast_or_general(sp, fast, general)

            @block.gpsimd
            def _(pool):
                def gather(rows, table, index, landed):
                    nc.gpsimd.indirect_dma_start(rows, None, dram[table], bass.IndirectOffsetOnAxis(ap=index, axis=0)
                                                 ).then_inc(landed, 16)

                def fast():
                    def step(i):
                        for k in range(BODY):
                            if k % GRP == 0:
                                pool.wait_ge(idx_ready[k // GRP], i + 1)
                            if k % 2 == 0:
                                at_least(pool, low_ready[k // 2], i)
                                hold(pool, passed[0])
                            gather(hrow[:, k, :], "h_tab", idx[:, k // GRP, k % GRP:k % GRP + 1], h_in[k])
                    step(0)
                    with pool.Fori(1, z.STEPS) as i:
                        step(i)

                def general():
                    with pool.Fori(0, z.NG) as g:
                        pool.wait_ge(g_set, g + 1)
                        hold(pool, passed[0])
                        for k in range(GRP):
                            gather(hrow[:, k, :], "h_tab", idx_g[:, k:k + 1], g_rows)
                            gather(hrow[:, GRP + k, :], "rg_tab", idx_g[:, GRP + k:GRP + k + 1], g_rows)

                fast_or_general(pool, fast, general)

            @block.scalar
            def _(act):
                nc.scalar.copy(t["acc_ext"][:, 0:z.NP // 2],
                               t["ident"][0:2, 2:3].to_broadcast((2, z.NP // 2))).then_inc(zeroed, 1)

                def fast():
                    def indices(i, g):
                        nc.scalar.copy(idx[:, g, :], t["src16"][:, ds(i * BODY + g * GRP, GRP)]).then_inc(idx_ready[g], 1)

                    def unload(i, g):
                        act.wait_ge(summed[2 * g + 1], i + 1)
                        at_least(act, part_turned[g], i)
                        nc.scalar.copy(part[:, g, :], ps_sum[g][:, 0:z.DM]).then_inc(part_ready[g], 1)

                    def split(i, q):
                        r, n = with_step(q - 2, i)
                        at_least(act, summed[r], n)
                        for c in range(2):
                            nc.scalar.activation(off[:, 2 * (q % 2) + c, :], t["iota"][:, :], ACT.Abs,
                                                 bias=t["minus_place"][:, ds(i * BODY + 2 * q + c, 1)]).then_inc(off_ready, 1)
                        act.wait_ge(off_ready, (i * PAIRS + q) * 2 + 2)
                        nc.scalar.activation(member[:, places(q), :], off[:, places(q), :], ACT.Relu, bias=1.0, scale=-1.0)
                        act.wait_ge(msg_ready[q], i + 1)
                        nc.scalar.copy(high[:, places(q), 0:z.DX], hrow[:, 2 * q:2 * q + 2, :]).then_inc(high_ready[q], 1)

                    def step(i, first, last):
                        split(i, 0)
                        if not first:
                            unload(i - 1, 0)
                        split(i, 1)
                        if not first:
                            unload(i - 1, 1)
                        if not last:
                            for k in range(GRP):
                                act.wait_ge(h_in[k], 16 * i + 16)
                            indices(i + 1, 0)
                        split(i, 2)
                        split(i, 3)
                        if not last:
                            for k in range(GRP, BODY):
                                act.wait_ge(h_in[k], 16 * i + 16)
                            indices(i + 1, 1)

                    indices(0, 0)
                    indices(0, 1)
                    over_steps(act, step)
                    unload(L, 0)
                    unload(L, 1)

                def general():
                    with act.Fori(0, z.NG * z.NT) as u:
                        act.wait_ge(g_sum, u + 1)
                        nc.scalar.copy(part[:, 0, :], ps_sum[0][:, 0:z.DM]).then_inc(g_part, 1)

                fast_or_general(act, fast, general)

            def turn(g):
                for a in range(2):
                    nc.tensor.transpose(ps_tr[g][:, a * P:a * P + P], part[:, g, a * P:a * P + P], t["ident"][:, :])
                return nc.tensor.transpose(ps_tr[g][0:2, D:D + P], part[:, g, D:z.DM], t["ident"][:, :])

            @block.tensor
            def _(pe):
                def fast():
                    def relate(i, q):
                        g = q // 2
                        if q % 2 == 0:
                            pe.wait_ge(one_ready[g], i + 1)
                        r, n = with_step(q - 2, i)
                        at_least(pe, msg_ready[r], n)
                        for c in range(2):
                            for k in range(z.KT):
                                for a in range(2):
                                    mm = nc.tensor.matmul(
                                        ps_rel[q % 2][:, c, 0:z.DM],
                                        one[:, g, k, ((q % 2) * 2 + c) * P:((q % 2) * 2 + c + 1) * P],
                                        t["table"][:, k, a, :], start=(k == 0 and a == 0), stop=(k == z.KT - 1 and a == 1))
                        mm.then_inc(rel_ready[q], 1)

                    def add(i, q):
                        g = q // 2
                        pe.wait_ge(high_ready[q], i + 1)
                        pe.wait_ge(low_ready[q], i + 1)
                        if q % 2 == 0:
                            at_least(pe, part_ready[g], i)
                        for c in range(2):
                            slot = 2 * (q % 2) + c
                            for a, half in enumerate((high, low)):
                                mm = nc.tensor.matmul(ps_sum[g][:, 0:z.DM], member[:, slot, :], half[:, slot, :],
                                                      start=(q % 2 == 0 and c == 0 and a == 0),
                                                      stop=(q % 2 == 1 and c == 1 and a == 1))
                        mm.then_inc(summed[q], 1)

                    def turned(i, g):
                        pe.wait_ge(part_ready[g], i + 1)
                        at_least(pe, added[g], 2 * i)
                        turn(g).then_inc(part_turned[g], 1)

                    def step(i, first, last):
                        relate(i, 0)
                        if not first:
                            add(i - 1, 2)
                        relate(i, 1)
                        if not first:
                            add(i - 1, 3)
                            turned(i - 1, 0)
                        relate(i, 2)
                        add(i, 0)
                        if not first:
                            turned(i - 1, 1)
                        relate(i, 3)
                        add(i, 1)

                    pe.wait_ge(consts, 2)
                    over_steps(pe, step)
                    add(L, 2)
                    add(L, 3)
                    turned(L, 0)
                    turned(L, 1)

                def general():
                    with pe.Fori(0, z.NG * z.NT) as u:
                        pe.wait_ge(g_member, u + 1)
                        for k in range(GRP):
                            for a, half in enumerate((high, low)):
                                mm = nc.tensor.matmul(ps_sum[0][:, 0:z.DM], member[:, k, :], half[:, k, :],
                                                      start=(k == 0 and a == 0), stop=(k == GRP - 1 and a == 1))
                        mm.then_inc(g_sum, 1)
                        pe.wait_ge(g_part, u + 1)
                        turn(0).then_inc(g_turned, 1)

                fast_or_general(pe, fast, general)

            @block.vector
            def _(dve):
                nc.vector.memset(high[:, :, z.DM - 1:z.DM].bitcast(F32), 1.0).then_inc(consts, 1)
                nc.vector.memset(low[:, :, z.DM - 1:z.DM].bitcast(F32), 0.0).then_inc(consts, 1)
                acc = t["acc"][:, :, :].rearrange("p a n -> p (a n)")
                nc.vector.memset(acc[:, z.NT * D:2 * z.ACCW], 0.0).then_inc(zeroed, 1)
                dve.wait_ge(consts, 2)
                nc.vector.memset(t["acc_ext"][:, z.NP // 2:z.ACCW], 0.0).then_inc(zeroed, 1)
                dve.wait_ge(zeroed, 3)

                def add_window(g, at, done):
                    nc.vector.tensor_tensor(t["acc"][:, :, ds(at, WIN)], ps_tr[g][:, 0:D].rearrange("p (a n) -> p a n", a=2),
                                            t["acc"][:, :, ds(at, WIN)], ALU.add).then_inc(done, 1)
                    nc.vector.tensor_tensor(t["acc_ext"][:, ds(at, WIN)], ps_tr[g][0:2, D:D + P],
                                            t["acc_ext"][:, ds(at, WIN)], ALU.add).then_inc(done, 1)

                def fast():
                    def onehots(i, g):
                        dve.wait_ge(typ_in[g], 16 * i + 16)
                        at_least(dve, rel_ready[2 * g + 1], i)
                        for k in range(z.KT):
                            last = nc.vector.tensor_scalar(one[:, g, k, :], typ_b[:, g, :], t["rel_id"][:, k:k + 1], None,
                                                           ALU.is_equal)
                        last.then_inc(one_ready[g], 1)

                    def multiply(i, q):
                        for k in (2 * q, 2 * q + 1):
                            dve.wait_ge(h_in[k], 16 * i + 16)
                        dve.wait_ge(rel_ready[q], i + 1)
                        rows = hrow[:, 2 * q:2 * q + 2, :]
                        nc.vector.tensor_tensor(rows, ps_rel[q % 2][:, :, 0:z.DX], rows, ALU.mult).then_inc(msg_ready[q], 1)

                    def rest(i, q):
                        dve.wait_ge(high_ready[q], i + 1)
                        nc.vector.tensor_tensor(low[:, places(q), 0:z.DX], hrow[:, 2 * q:2 * q + 2, :],
                                                high[:, places(q), 0:z.DX].bitcast(F32), ALU.subtract).then_inc(low_ready[q], 1)

                    def add(i, g):
                        at = dve.value_load(t["base_id"][0:1, ds(2 * i + g, 1)], min_val=0, max_val=z.NP)
                        dve.wait_ge(part_turned[g], i + 1)
                        if g == 0:
                            at_least(dve, added[1], 2 * i)
                        else:
                            dve.wait_ge(added[0], 2 * i + 2)
                        add_window(g, at, added[g])

                    def step(i, first, last):
                        multiply(i, 0)
                        if not first:
                            rest(i - 1, 3)
                        multiply(i, 1)
                        rest(i, 0)
                        if not first:
                            add(i - 1, 0)
                        if not last:
                            onehots(i + 1, 0)
                        multiply(i, 2)
                        rest(i, 1)
                        if not first:
                            add(i - 1, 1)
                        multiply(i, 3)
                        rest(i, 2)
                        if not last:
                            onehots(i + 1, 1)

                    onehots(0, 0)
                    onehots(0, 1)
                    over_steps(dve, step)
                    rest(L, 3)
                    add(L, 0)
                    add(L, 1)

                def general():
                    def group(g):
                        dve.wait_ge(g_in, 32 * g + 32)
                        nc.vector.tensor_copy(place_g[:, :], dst_g[:, :]).then_inc(g_place, 1)
                        nc.vector.tensor_copy(idx_g[:, 0:GRP], t["src16"][:, ds(g * GRP, GRP)])
                        nc.vector.tensor_copy(idx_g[:, GRP:2 * GRP], typ_g[:, :]).then_inc(g_set, 1)
                        dve.wait_ge(g_rows, (g + 1) * (2 * GRP * 16))
                        rows = hrow[:, 0:GRP, :]
                        nc.vector.tensor_tensor(rows, rows, hrow[:, GRP:2 * GRP, :], ALU.mult).then_inc(g_msg, 1)
                        dve.wait_ge(g_msg, g + 1)
                        hold(dve, passed[2])
                        nc.vector.tensor_copy(high[:, :, 0:z.DX], rows).then_inc(g_high, 1)
                        dve.wait_ge(g_high, g + 1)
                        nc.vector.tensor_tensor(low[:, :, 0:z.DX], rows, high[:, :, 0:z.DX].bitcast(F32),
                                                ALU.subtract).then_inc(g_low, 1)
                        dve.wait_ge(g_low, g + 1)
                        hold(dve, passed[2])
                        with dve.Fori(0, z.NT) as w:
                            u = g * z.NT + w
                            dve.wait_ge(g_place, g * (z.NT + 1) + w + 1)
                            for k in range(GRP):
                                last = nc.vector.tensor_scalar(member[:, k, :], t["iota"][:, :], place_g[:, k:k + 1], None,
                                                               ALU.is_equal)
                            last.then_inc(g_member, 1)
                            dve.wait_ge(g_member, u + 1)
                            nc.vector.tensor_scalar(place_g[:, :], place_g[:, :], -float(WIN), None,
                                                    ALU.add).then_inc(g_place, 1)
                            dve.wait_ge(g_turned, u + 1)
                            add_window(0, w * WIN, g_added)
                            dve.wait_ge(g_added, 2 * u + 2)
                            hold(dve, passed[2])

                    with dve.Fori(0, z.NG) as g:
                        group(g)

                fast_or_general(dve, fast, general)


def stage_5(nc, z, dram, t, out):
    ctx = ExitStack()
    with ctx:
        def sb(name, shape, dt):
            return ctx.enter_context(nc.sbuf_tensor(name, shape, dt))

        def sem(name):
            return t["sems"].enter_context(nc.semaphore(name))

        LOT = 7
        L = z.NT // LOT - 1
        ext_rows = sb("ext_rows", [z.NT, 2, P], F32)
        norm = sb("in_norm", [P, z.NT], F32)
        b_norm = sb("b_norm", [P, z.NT], F32)
        one_row = sb("one_row", [1, P], F32)
        w_ext = sb("w_ext_rows", [P, D], F32)
        a_tile = sb("a_tile", [P, LOT, 2, P], F32)
        row = sb("row", [P, LOT, D], F32)
        done_row = sb("done_row", [P, LOT, D], F32)
        ps = [ctx.enter_context(nc.psum_tensor(f"ps_final{n}", [P, 512], F32)) for n in range(LOT)]
        ps_ext = ctx.enter_context(nc.psum_tensor("ps_ext", [P, 512], F32))
        deg_out = sem("ext_stored")
        deg_in = sem("ext_loaded")
        deg_turned = sem("ext_turned")
        ones_set = sem("one_row_set")
        deg_ready = sem("in_deg_clamped")
        root_ready = sem("in_deg_root")
        norm_ready = sem("in_norm_ready")
        row_in = [sem(f"row_in{s}") for s in range(LOT)]
        tile_ready = sem("tile_ready")
        product = sem("product")
        b_added = sem("b_added")
        row_done = sem("row_done")
        row_out = [sem(f"final_stored{s}") for s in range(LOT)]
        passed = [sem(f"stage5_{n}_passed") for n in ("sp", "pool")]

        def over_steps(eng, step):
            step(0)
            with eng.Fori(1, L + 1) as i:
                step(i)

        with nc.Block() as block:
            @block.sync
            def _(sp):
                sp.dma_start(dram["ext"], t["acc_ext"][:, 0:z.NP]).then_inc(deg_out, 16)
                sp.wait_ge(deg_out, 16)
                sp.dma_start(ext_rows[:, :, :], dram["ext"].rearrange("e (t p) -> t e p", p=P)).then_inc(deg_in, 16)

                def step(i):
                    for s in range(LOT):
                        at_least(sp, row_done, (i - 1) * LOT + s + 1)
                        hold(sp, passed[0])
                        sp.dma_start(row[:, s, :], dram["base_out"][ds((i * LOT + s) * P, P), :]).then_inc(row_in[s], 16)
                over_steps(sp, step)

            @block.gpsimd
            def _(pool):
                def store(i, s, rows):
                    pool.wait_ge(row_done, i * LOT + s + 1)
                    hold(pool, passed[1])
                    pool.dma_start(out[ds((i * LOT + s) * P, rows), :], done_row[0:rows, s, :]).then_inc(row_out[s], 16)

                with pool.Fori(0, L) as i:
                    for s in range(LOT):
                        store(i, s, P)
                for s in range(LOT - 1):
                    store(L, s, P)
                store(L, LOT - 1, z.LAST)
                for s in range(LOT):
                    pool.wait_ge(row_out[s], 16 * (L + 1))

            @block.scalar
            def _(act):
                def step(i):
                    for s in range(LOT):
                        at_least(act, product, (i - 1) * LOT + s + 1)
                        nodes = ds((i * LOT + s) * P, P)
                        nc.scalar.copy(a_tile[:, s, :, :], t["acc"][:, :, nodes]).then_inc(tile_ready, 1)
                step(0)
                act.wait_ge(deg_ready, 1)
                nc.scalar.activation(norm[:, :], norm[:, :], ACT.Sqrt).then_inc(root_ready, 1)
                with act.Fori(1, L + 1) as i:
                    step(i)

            @block.tensor
            def _(pe):
                pe.wait_ge(ones_set, 1)
                nc.tensor.matmul(ps_ext[:, 256:256 + D], one_row[:, :], t["w_ext"][:, :], start=True, stop=True)
                pe.wait_ge(deg_in, 16)
                for e in range(2):
                    mm = nc.tensor.transpose(ps_ext[:, e * P:e * P + z.NT], ext_rows[:, e, :], t["ident"][0:z.NT, 0:z.NT])
                mm.then_inc(deg_turned, 1)

                def step(i):
                    for s in range(LOT):
                        pe.wait_ge(tile_ready, i * LOT + s + 1)
                        at_least(pe, row_done, (i - 1) * LOT + s + 1)
                        for a in range(2):
                            mm = nc.tensor.matmul(ps[s][:, 0:D], a_tile[:, s, a, :], t["w_agg"][:, a, :],
                                                  start=(a == 0), stop=(a == 1))
                        mm.then_inc(product, 1)
                over_steps(pe, step)

            @block.vector
            def _(dve):
                nc.vector.memset(one_row[:, :], 1.0).then_inc(ones_set, 1)
                dve.wait_ge(deg_turned, 1)
                nc.vector.tensor_scalar(norm[:, :], ps_ext[:, P:P + z.NT], 1.0, None, ALU.max).then_inc(deg_ready, 1)
                nc.vector.tensor_copy(w_ext[:, :], ps_ext[:, 256:256 + D]).then_inc(norm_ready, 1)
                dve.wait_ge(root_ready, 1)
                nc.vector.reciprocal(norm[:, :], norm[:, :]).then_inc(norm_ready, 1)
                dve.wait_ge(norm_ready, 2)
                nc.vector.tensor_tensor(b_norm[:, :], ps_ext[:, 0:z.NT], norm[:, :], ALU.mult).then_inc(norm_ready, 1)
                dve.wait_ge(norm_ready, 3)

                def step(i):
                    for s in range(LOT):
                        dve.wait_ge(row_in[s], 16 * i + 16)
                        nc.vector.scalar_tensor_tensor(out=row[:, s, :], in0=w_ext[:, :],
                                                       scalar=b_norm[:, ds(i * LOT + s, 1)], in1=row[:, s, :],
                                                       op0=ALU.mult, op1=ALU.add).then_inc(b_added, 1)
                    for s in range(LOT):
                        dve.wait_ge(product, i * LOT + s + 1)
                        dve.wait_ge(b_added, i * LOT + s + 1)
                        at_least(dve, row_out[s], 16 * i)
                        nc.vector.scalar_tensor_tensor(out=done_row[:, s, :], in0=ps[s][:, 0:D],
                                                       scalar=norm[:, ds(i * LOT + s, 1)], in1=row[:, s, :],
                                                       op0=ALU.mult, op1=ALU.add).then_inc(row_done, 1)
                over_steps(dve, step)


def gnn_layer(nc, io, out):
    z = Sizes(io["x"].shape[0], io["src"].shape[0], io["rel"].shape[0])
    dram = {
        "h_tab": nc.dram_tensor("h_tab", [z.NP, z.DX], F32).ap(),
        "rg_tab": nc.dram_tensor("rg_tab", [z.R, z.DX], F32).ap(),
        "base_out": nc.dram_tensor("base_out", [z.NP, D], F32).ap(),
        "typ_row": nc.dram_tensor("typ_row", [z.NB * P * P], F16).ap(),
        "typ_cols": nc.dram_tensor("typ_cols", [P, z.CH], I16).ap(),
        "dst_cols": nc.dram_tensor("dst_cols", [P, z.CH], I16).ap(),
        "ext": nc.dram_tensor("ext", [2, z.NP], F32).ap(),
    }
    with ExitStack() as keep:
        t = {"sems": keep}

        def sb(ctx, name, shape, dt):
            t[name] = ctx.enter_context(nc.sbuf_tensor(name, shape, dt))

        sb(keep, "acc", [P, 2, z.ACCW], F32)
        t["x_all"] = t["acc"][:, :, :].rearrange("p a n -> p (a n)")[:, 0:z.NT * D].rearrange("p (t d) -> p t d", d=D)
        sb(keep, "ident", [P, P], F32)
        sb(keep, "iota", [P, P], F32)
        sb(keep, "eps", [P, 1], F32)
        sb(keep, "rel_id", [P, z.KT], F32)
        sb(keep, "src16", [P, z.CH], I16)
        sb(keep, "minus_place", [P, z.CH], F16)
        sb(keep, "table", [P, z.KT, 2, z.DM], F32R)
        sb(keep, "w_agg", [P, 2, D], F32)
        sb(keep, "w_ext", [1, D], F32)
        sb(keep, "base_id", [1, z.NG], I32)
        sb(keep, "flag", [1, 1], I32)
        x_in = keep.enter_context(nc.semaphore("x_in"))
        with ExitStack() as early:
            sb(early, "ones", [P, P], F32)
            sb(early, "iota_k", [P, P, COUNT], BF16)
            sb(early, "src_lo", [P, z.CH], BF16)
            sb(early, "src_hi", [P, z.CH], BF16)
            sb(early, "upd_k", [P, 2, D], F32)
            sb(early, "upd_b2", [2, D], F32R)
            sb(early, "minus_ones", [2, P], F32R)
            sb(early, "rstd", [P, z.NT], F32)
            sb(early, "shift", [P, z.NT], F32)
            sb(early, "src_norm", [P, z.NT], F32)
            stage_1(nc, z, io, dram, t, x_in)
            stage_2(nc, z, dram, t, x_in)
            stage_3(nc, z, dram, t)
        with ExitStack() as late:
            sb(late, "acc_ext", [2, z.ACCW], F32)
            stage_4(nc, z, dram, t)
            stage_5(nc, z, dram, t, out)


def kernel(x, src, dst, edge_type_500, L0_gnn_relation_emb, L0_gnn_msg_w, L0_gnn_msg_b, L0_gnn_upd_w, L0_gnn_upd_b,
           L0_gnn_gate_w, L0_gnn_gate_b):
    import numpy as np
    import concourse.bacc as bacc
    from concourse.bass_utils import run_bass_kernel_spmd

    laid_out = {
        "x": np.asarray(x),
        "src": np.asarray(src),
        "dst": np.asarray(dst),
        "typ": np.asarray(edge_type_500),
        "rel": np.asarray(L0_gnn_relation_emb),
        "msg_w": np.asarray(L0_gnn_msg_w).transpose(1, 0, 2),
        "msg_b": np.asarray(L0_gnn_msg_b).reshape(2, P).T,
        "upd_w": np.asarray(L0_gnn_upd_w).transpose(2, 1, 0),
        "upd_b": np.asarray(L0_gnn_upd_b).T.reshape(1, D),
        "gate_w": np.asarray(L0_gnn_gate_w).reshape(C, BL).T.reshape(1, D),
        "gate_b": np.asarray(L0_gnn_gate_b).reshape(1, 1),
    }
    nc = bacc.Bacc("TRN2", target_bir_lowering=False, num_devices=1)
    arrays, io = {}, {}
    for name, a in laid_out.items():
        arrays[f"in_{name}"] = np.ascontiguousarray(a)
        io[name] = nc.dram_tensor(f"in_{name}", a.shape, mybir.dt.from_np(a.dtype), kind="ExternalInput").ap()
    out = nc.dram_tensor("out", laid_out["x"].shape, F32, kind="ExternalOutput").ap()
    gnn_layer(nc, io, out)
    result = run_bass_kernel_spmd(nc, [arrays], core_ids=[0])
    return result.results[0]["out"]
```

```python
from contextlib import ExitStack

import concourse.bass as bass
from concourse import mybir

ALU = mybir.AluOpType
ACT = mybir.ActivationFunctionType
AX = mybir.AxisListType
F32 = mybir.dt.float32
F32R = mybir.dt.float32r
F16 = mybir.dt.float16
BF16 = mybir.dt.bfloat16
I32 = mybir.dt.int32
I16 = mybir.dt.int16
ds = bass.ds

P = 128
D = 256
C = 64
BL = 4
EPS = 1e-5
GRP = 4
BODY = 8
COUNT = 16
WIN = 128
PAD_ID = 16383
BLADE = [[0, 1, 2, 3], [1, 0, 3, 2], [2, 3, 0, 1], [3, 2, 1, 0]]
SIGN = [[1, 1, 1, -1], [1, 1, -1, 1], [1, 1, 1, -1], [1, 1, 1, 1]]


def at_least(eng, sem, value):
    if isinstance(value, int) and value <= 0:
        return
    eng.wait_ge(sem, value)


def hold(eng, passed):
    eng.sem_inc(passed, 1)


class Sizes:

    def __init__(self, n, e, r):
        self.N, self.E, self.R = n, e, r
        self.NT = -(-n // P)
        self.LAST = n - (self.NT - 1) * P
        self.NP = self.NT * P
        self.STEPS = -(-e // (P * BODY))
        self.CH = self.STEPS * BODY
        self.NG = self.CH // GRP
        self.NB = -(-self.CH // P)
        self.CB = self.CH - (self.NB - 1) * P
        self.FULL = e // P - (self.NB - 1) * P
        self.REST = e % P
        self.KT = -(-r // P)
        self.RL = r - (self.KT - 1) * P
        self.DX = D + 1
        self.DM = D + 2
        assert self.STEPS % 2 == 0
        self.PER = self.CH // self.NT
        assert self.NT % 14 == 0 and self.NP <= 16000 and r <= 2048
        assert self.PER * self.NT == self.CH and self.PER == COUNT and 0 < self.FULL < P and self.KT > 1


def stage_1(nc, z, io, dram, t, x_in, stored):
    ctx = ExitStack()
    with ctx:
        def sb(name, shape, dt):
            return ctx.enter_context(nc.sbuf_tensor(name, shape, dt))

        def sem(name):
            return t["sems"].enter_context(nc.semaphore(name))

        lists = ["src", "dst", "typ"]
        rows_i = [sb(f"rows_i_{n}", [P, z.NB, P], I32) for n in lists]
        rows_f = [r[:, :, :].bitcast(F32) for r in rows_i]
        cols = [sb(f"cols_{n}", [P, z.CH], F32) for n in lists]
        base = sb("base", [P, z.NG], F32)
        whole, digit = (rows_i[0][:, :, :].rearrange("p b j -> p (b j)")[:, 0:z.CH],
                        rows_i[1][:, :, :].rearrange("p b j -> p (b j)")[:, 0:z.CH])
        ones = sb("ones", [P, P], F32)
        far, here = cols[0], cols[2]
        digit_f = rows_f[2].rearrange("p b j -> p (b j)")[:, 0:z.CH]
        pads = rows_f[0].rearrange("p b j -> p (b j)")[:, 0:z.CH]
        base_i = sb("base_i", [P, z.NG], I32)
        base_low = sb("base_low", [P, z.NG], I32)
        base_f = sb("base_f", [P, z.NG], F32)
        bad = sb("bad", [P, 1], F32)
        upd_w = sb("upd_w", [P, C, BL], F32)
        msg_w = sb("msg_w", [P, BL, C], F32)
        msg_k = sb("msg_k", [P, 2, D], F32)
        msg_b = sb("msg_b", [P, 2], F32)
        upd_b = sb("upd_b", [2, D], F32)
        upd_b_high = sb("upd_b_high", [2, D], F32R)
        rel = sb("rel", [P, z.KT, D], F32)
        gate_w = sb("gate_w", [P, D], F32)
        gate_b = sb("gate_b", [P, 1], F32)
        logit = sb("logit", [P, z.KT], F32)
        gate = sb("gate", [P, z.KT], F32)
        rows_h, col16, gated, w_agg = t["rows_h"], [t["dst16"], t["typ16"]], t["gated"], t["w_agg"]
        prod = gated
        pt = [ctx.enter_context(nc.psum_tensor(f"turn{n}", [P, 512], F32)) for n in range(8)]

        pads_set = sem("pads_set")
        consts_set = sem("consts_set")
        iotas_set = sem("iotas_set")
        list_in = [sem(f"in_{n}") for n in lists]
        cast = sem("lists_cast")
        half_cast = sem("typ_half_cast")
        turned = sem("turned")
        unloaded = [sem(f"turn_unloaded_{n}") for n in lists]
        cols_ready = sem("cols_ready")
        base_ps = sem("base_in_psum")
        chain = sem("vector_chain")
        bad_ready = sem("bad_ready")
        bad_ps = sem("bad_in_psum")
        w_in = sem("weights_in")
        w_built = sem("weights_built")
        w_ps = sem("weights_in_psum")
        w_ready = sem("w_agg_ready")
        rel_zero = sem("rel_zeroed")
        rel_in = sem("rel_in")
        logit_ready = sem("logit_ready")
        gate_ready = sem("gate_ready")
        gated_ready = sem("gated_ready")
        x_zero = sem("x_zeroed")

        banks = [list(range(b, min(b + 4, z.NB))) for b in range(0, z.NB, 4)]
        assert len(banks) == 4

        def unload(eng, copy, n):
            for b, blocks in enumerate(banks):
                eng.wait_ge(turned, 4 * n + b + 1)
                width = min(4 * P, z.CH - b * 4 * P)
                copy(cols[n][:, b * 4 * P:b * 4 * P + width], pt[4 * (n % 2) + b][:, 0:width]).then_inc(unloaded[n], 1)

        with nc.Block() as block:
            @block.sync
            def _(sp):
                sp.wait_ge(pads_set, 3)
                for n, arr in enumerate((io["src"], io["dst"], io["typ"])):
                    full = (z.NB - 1) * P * P
                    sp.dma_start(rows_i[n][:, 0:z.NB - 1, :],
                                 arr[0:full].rearrange("(b p j) -> p b j", p=P, j=P)).then_inc(list_in[n], 16)
                    sp.dma_start(rows_i[n][0:z.FULL, z.NB - 1, :],
                                 arr[full:full + z.FULL * P].rearrange("(p j) -> p j", j=P)).then_inc(list_in[n], 16)
                    sp.dma_start(rows_i[n][z.FULL:z.FULL + 1, z.NB - 1, 0:z.REST],
                                 arr[z.E - z.REST:z.E].rearrange("(p j) -> p j", p=1)).then_inc(list_in[n], 16)
                for h in range(2):
                    sp.dma_start(upd_w[C * h:C * h + C, :, :], io["upd_w"]).then_inc(w_in, 16)
                    sp.dma_start(msg_w[C * h:C * h + C, :, :], io["msg_w"]).then_inc(w_in, 16)
                sp.dma_start(msg_b[:, :], io["msg_b"]).then_inc(w_in, 16)
                sp.dma_start(upd_b[:, :], io["upd_b"].to_broadcast((2, D))).then_inc(w_in, 16)
                sp.wait_ge(rel_zero, 1)
                sp.dma_start(rel[:, 0:z.KT - 1, :],
                             io["rel"][0:(z.KT - 1) * P, :].rearrange("(k p) d -> p k d", p=P)).then_inc(rel_in, 16)
                sp.dma_start(rel[0:z.RL, z.KT - 1, :], io["rel"][(z.KT - 1) * P:z.R, :]).then_inc(rel_in, 16)
                sp.dma_start(gate_w[:, :], io["gate_w"].to_broadcast((P, D))).then_inc(rel_in, 16)
                sp.dma_start(gate_b[:, :], io["gate_b"].to_broadcast((P, 1))).then_inc(rel_in, 16)
                sp.wait_ge(x_zero, 1)
                for c in range(0, z.NT - 14, 14):
                    sp.dma_start(t["x_all"][:, c:c + 14, :],
                                 io["x"][c * P:(c + 14) * P, :].rearrange("(t p) d -> p t d", p=P)).then_inc(x_in, 16)
                c = z.NT - 14
                sp.dma_start(t["x_all"][:, c:c + 13, :],
                             io["x"][c * P:(c + 13) * P, :].rearrange("(t p) d -> p t d", p=P)).then_inc(x_in, 16)
                sp.dma_start(t["x_all"][0:z.LAST, z.NT - 1, :], io["x"][z.NP - P:z.N, :]).then_inc(x_in, 16)

            @block.scalar
            def _(act):
                act.wait_ge(cast, 3)
                nc.scalar.copy(rows_h[:, :, :], rows_f[2]).then_inc(half_cast, 1)
                act.wait_ge(w_in, 96)
                upd_cols = t["upd_k"][:, :, :].rearrange("p h (c b) -> p h c b", b=BL)
                for i in range(BL):
                    for j in range(BL):
                        p0 = C * (j % 2)
                        nc.scalar.mul(upd_cols[p0:p0 + C, j // 2, :, i], upd_w[p0:p0 + C, :, BLADE[i][j]],
                                      float(SIGN[i][j])).then_inc(w_built, 1)
                        p0 = C * (i % 2)
                        nc.scalar.mul(msg_k[p0:p0 + C, i // 2, C * j:C * j + C], msg_w[p0:p0 + C, BLADE[i][j], :],
                                      float(SIGN[i][j])).then_inc(w_built, 1)
                act.wait_ge(logit_ready, 1)
                nc.scalar.activation(gate[:, :], logit[:, :], ACT.Sigmoid, bias=gate_b[:, :]).then_inc(gate_ready, 1)
                unload(act, nc.scalar.copy, 1)
                unload(act, nc.scalar.copy, 2)
                act.wait_ge(unloaded[1], 4)
                nc.scalar.copy(col16[0][:, :], cols[1][:, :]).then_inc(cols_ready, 1)
                act.wait_ge(half_cast, 1)
                act.dma_start(dram["typ_row"].rearrange("(b p j) -> p b j", p=P, j=P), rows_h[:, :, :]).then_inc(stored, 16)
                act.wait_ge(cols_ready, 2)
                act.dma_start(dram["dst_cols"], col16[0][:, :]).then_inc(stored, 16)
                act.dma_start(dram["typ_cols"], col16[1][:, :]).then_inc(stored, 16)
                act.wait_ge(gated_ready, 2 * z.KT + 1)
                act.dma_start(dram["rg_tab"][0:(z.KT - 1) * P, :].rearrange("(k p) d -> p k d", p=P),
                              gated[:, 0:z.KT - 1, 0:z.DX]).then_inc(stored, 16)
                act.dma_start(dram["rg_tab"][(z.KT - 1) * P:z.R, :],
                              gated[0:z.RL, z.KT - 1, 0:z.DX]).then_inc(stored, 16)
                act.wait_ge(w_ready, 1)
                act.dma_start(dram["w_agg"].rearrange("h p d -> p h d"), w_agg[:, :, :]).then_inc(stored, 16)

            @block.gpsimd
            def _(pool):
                for n in range(3):
                    nc.gpsimd.memset(rows_i[n][:, z.NB - 1, :], PAD_ID).then_inc(pads_set, 1)
                nc.gpsimd.memset(rel[:, z.KT - 1, :], 0.0).then_inc(rel_zero, 1)
                nc.gpsimd.memset(t["x_all"][:, z.NT - 1, :], 0.0).then_inc(x_zero, 1)
                nc.gpsimd.memset(t["ident"][:, :], 0.0).then_inc(consts_set, 1)
                nc.gpsimd.memset(ones[:, :], 1.0).then_inc(consts_set, 1)
                nc.gpsimd.memset(t["minus_ones"][:, :].bitcast(F32), -1.0).then_inc(consts_set, 1)
                nc.gpsimd.memset(t["eps"][:, :], EPS).then_inc(consts_set, 1)
                pool.wait_ge(consts_set, 1)
                nc.gpsimd.affine_select(out=t["ident"][:, :], in_=t["ident"][:, :], compare_op=ALU.not_equal, fill=1.0,
                                        base=0, pattern=[[-1, P]], channel_multiplier=1).then_inc(iotas_set, 1)
                nc.gpsimd.iota(t["iota"][:, :], [[1, P]], base=0, channel_multiplier=0,
                               allow_small_or_imprecise_dtypes=True).then_inc(iotas_set, 1)
                nc.gpsimd.iota(t["iota_k"][:, :, :], [[1, P], [0, COUNT]], base=0, channel_multiplier=0,
                               allow_small_or_imprecise_dtypes=True).then_inc(iotas_set, 1)
                nc.gpsimd.iota(t["rel_id"][:, :], [[P, z.KT]], base=0, channel_multiplier=1,
                               allow_small_or_imprecise_dtypes=True).then_inc(iotas_set, 1)

            @block.tensor
            def _(pe):
                pe.wait_ge(iotas_set, 1)
                pe.wait_ge(consts_set, 2)
                for n in range(3):
                    pe.wait_ge(cast, n + 1)
                    for b, blocks in enumerate(banks):
                        if n == 2:
                            pe.wait_ge(unloaded[0], b + 1)
                        for k, blk in enumerate(blocks):
                            rows = P if blk < z.NB - 1 else z.CB
                            mm = nc.tensor.transpose(pt[4 * (n % 2) + b][:, k * P:k * P + rows],
                                                     rows_f[n][0:rows, blk, :], t["ident"][0:rows, 0:rows])
                        mm.then_inc(turned, 1)
                pe.wait_ge(unloaded[1], 4)
                nc.tensor.matmul(pt[4][:, 0:z.NG], ones[0:1, :], cols[1][0:1, 0:z.CH:GRP],
                                 start=True, stop=True).then_inc(base_ps, 1)
                pe.wait_ge(w_built, 2 * BL * BL)
                for i in range(2):
                    for m in range(2):
                        nc.tensor.matmul(pt[5][:, i * D:i * D + D], msg_k[:, m, i * P:i * P + P], t["upd_k"][:, m, :],
                                         start=(m == 0), stop=(m == 1))
                for m in range(2):
                    mm = nc.tensor.matmul(pt[6][0:1, 0:D], msg_b[:, m:m + 1], t["upd_k"][:, m, :],
                                          start=(m == 0), stop=(m == 1))
                mm.then_inc(w_ps, 1)
                pe.wait_ge(bad_ready, 1)
                nc.tensor.matmul(pt[7][0:1, 0:1], bad[:, :], ones[:, 0:1], start=True, stop=True).then_inc(bad_ps, 1)

            @block.vector
            def _(dve):
                links = [0]

                def link(ins):
                    links[0] += 1
                    ins.then_inc(chain, 1)
                    dve.wait_ge(chain, links[0])

                for n in range(3):
                    dve.wait_ge(list_in[n], 48)
                    nc.vector.tensor_copy(rows_f[n], rows_i[n][:, :, :]).then_inc(cast, 1)
                dve.wait_ge(rel_in, 64)
                for k in range(z.KT):
                    nc.vector.tensor_tensor(prod[:, k, 0:D], rel[:, k, :], gate_w[:, :], ALU.mult).then_inc(chain, 1)
                links[0] += z.KT
                dve.wait_ge(chain, links[0])
                nc.vector.tensor_reduce(logit[:, :], prod[:, :, 0:D], AX.X, ALU.add).then_inc(logit_ready, 1)

                unload(dve, nc.vector.tensor_copy, 0)
                dve.wait_ge(unloaded[0], 4)
                dve.wait_ge(turned, 8)
                nc.vector.tensor_scalar(t["src16"][:, :], cols[0][:, :], float(z.N - 1), None, ALU.min).then_inc(chain, 1)
                links[0] += 1
                link(nc.vector.tensor_copy(whole[:, :], cols[0][:, :]))
                link(nc.vector.tensor_scalar(digit[:, :], whole[:, :], P - 1, None, ALU.bitwise_and))
                link(nc.vector.tensor_copy(t["src_lo"][:, :], digit[:, :]))
                link(nc.vector.tensor_scalar(digit[:, :], whole[:, :], 7, None, ALU.arith_shift_right))
                link(nc.vector.tensor_copy(t["src_hi"][:, :], digit[:, :]))
                dve.wait_ge(unloaded[2], 4)
                nc.vector.tensor_scalar(col16[1][:, :], cols[2][:, :], float(z.R - 1), None, ALU.min).then_inc(cols_ready, 1)
                dve.wait_ge(cols_ready, 2)
                dve.wait_ge(base_ps, 1)
                link(nc.vector.tensor_scalar(base[:, :], pt[4][:, 0:z.NG], float(z.NP - 1), 0.0, ALU.min, ALU.max))
                link(nc.vector.tensor_copy(base_i[:, :], base[:, :]))
                link(nc.vector.tensor_scalar(t["tile_id"][:, :], base_i[0:1, :], 7, None, ALU.arith_shift_right))
                link(nc.vector.tensor_scalar(base_low[:, :], base_i[:, :], P - 1, None, ALU.bitwise_and))
                link(nc.vector.tensor_copy(base_f[:, :], base_low[:, :]))
                dve.wait_ge(iotas_set, 4)
                link(nc.vector.tensor_scalar(t["mask"][:, 0, :], base_f[:, :], t["rel_id"][:, 0:1], None, ALU.is_le))
                link(nc.vector.tensor_scalar(t["mask"][:, 1, :], base_f[:, :], t["rel_id"][:, 0:1], None, ALU.is_gt))
                link(nc.vector.tensor_tensor(far[:, :].rearrange("p (g k) -> p g k", k=GRP),
                                             cols[1][:, :].rearrange("p (g k) -> p g k", k=GRP),
                                             base[:, :].to_broadcast((P, z.NG, GRP)), ALU.subtract))
                link(nc.vector.tensor_scalar(here[:, :], cols[1][:, :], float(PAD_ID), None, ALU.is_lt))
                link(nc.vector.tensor_copy(whole[:, :], cols[1][:, :]))
                link(nc.vector.tensor_scalar(digit[:, :], whole[:, :], P - 1, None, ALU.bitwise_and))
                dve.wait_ge(half_cast, 1)
                link(nc.vector.tensor_copy(digit_f[:, :], digit[:, :]))
                link(nc.vector.tensor_scalar(pads[:, :], cols[1][:, :], float(PAD_ID), -2000.0, ALU.is_ge, ALU.mult))
                link(nc.vector.tensor_tensor(t["minus_place"][:, :], pads[:, :], digit_f[:, :], ALU.subtract))
                nc.vector.tensor_scalar(cols[1][:, :], far[:, :], 0.0, None, ALU.is_lt).then_inc(chain, 1)
                links[0] += 1
                link(nc.vector.tensor_scalar(far[:, :], far[:, :], float(WIN), None, ALU.is_ge))
                link(nc.vector.tensor_tensor(far[:, :], far[:, :], here[:, :], ALU.mult))
                link(nc.vector.tensor_tensor(far[:, :], far[:, :], cols[1][:, :], ALU.add))
                nc.vector.tensor_reduce(bad[:, :], far[:, :], AX.X, ALU.add).then_inc(bad_ready, 1)
                dve.wait_ge(gate_ready, 1)
                for k in range(z.KT):
                    nc.vector.tensor_scalar(gated[:, k, 0:D], rel[:, k, :], gate[:, k:k + 1], None,
                                            ALU.mult).then_inc(gated_ready, 1)
                    nc.vector.tensor_copy(gated[:, k, D:D + 1], gate[:, k:k + 1]).then_inc(gated_ready, 1)
                nc.vector.memset(gated[:, :, D + 1:D + 2], 0.0).then_inc(gated_ready, 1)
                dve.wait_ge(gated_ready, 2 * z.KT + 1)
                link(nc.vector.tensor_copy(t["table"][:, :, 0, :], gated[:, :, :]))
                link(nc.vector.tensor_tensor(t["table"][:, :, 1, :], gated[:, :, :],
                                             t["table"][:, :, 0, :].bitcast(F32), ALU.subtract))
                dve.wait_ge(iotas_set, 4)
                dve.wait_ge(w_in, 96)
                link(nc.vector.tensor_copy(upd_b_high[:, :], upd_b[:, :]))
                link(nc.vector.scalar_tensor_tensor(out=t["upd_b2"][:, :], in0=upd_b_high[:, :].bitcast(F32),
                                                    scalar=t["rel_id"][0:2, 0:1], in1=upd_b[:, :],
                                                    op0=ALU.mult, op1=ALU.subtract))
                dve.wait_ge(w_ps, 1)
                nc.vector.tensor_copy(w_agg[:, :, :], pt[5][:, :].rearrange("p (h d) -> p h d", h=2)).then_inc(w_ready, 1)
                link(nc.vector.tensor_copy(t["w_ext"][:, :], pt[6][0:1, 0:D]))
                dve.wait_ge(bad_ps, 1)
                link(nc.vector.tensor_copy(t["flag"][:, :], pt[7][0:1, 0:1]))


def stage_2(nc, z, dram, t, x_in, stored):
    ctx = ExitStack()
    with ctx:
        def sb(name, shape, dt):
            return ctx.enter_context(nc.sbuf_tensor(name, shape, dt))

        def sem(name):
            return t["sems"].enter_context(nc.semaphore(name))

        SLOT = COUNT
        SLOTS = 7
        HI = z.NT
        one_lo = sb("one_lo", [P, SLOTS, P, SLOT], BF16)
        one_hi = sb("one_hi", [P, SLOTS, HI, SLOT], BF16)
        zero_b = sb("zero_b", [P, P], BF16)
        work = sb("work", [P, 4, D], F32)
        stats = work[:, :, :].rearrange("p a d -> p (a d)")[:, 0:z.NT * 6].rearrange("p (t c) -> p t c", c=6)
        mean = sb("mean", [P, z.NT], F32)
        half = t["shift"]
        var = sb("var", [P, z.NT], F32)
        std = var
        h = sb("h", [P, 2, D], F32)
        h_t, base_row = work[:, 0:2, :], work[:, 2:4, :]
        deg = t["src_norm"]
        ps_turn = [ctx.enter_context(nc.psum_tensor(f"ps_turn{n}", [P, 512], F32)) for n in range(2)]
        ps_out = [ctx.enter_context(nc.psum_tensor(f"ps_out{n}", [P, 512], F32)) for n in range(2)]
        ps_deg = ctx.enter_context(nc.psum_tensor("ps_deg", [P, 512], F32))

        stats_ready = sem("stats_ready")
        moments = sem("moments")
        var_ready = sem("var_ready")
        std_ready = sem("std_ready")
        norm_ready = sem("norm_ready")
        onehots = sem("onehots_ready")
        counted = sem("onehots_counted")
        h_ready = [sem(f"h_ready{n}") for n in range(2)]
        turned = [sem(f"h_turned{n}") for n in range(2)]
        t_ready = [sem(f"h_t_ready{n}") for n in range(2)]
        summed = [sem(f"row_summed{n}") for n in range(2)]
        row_ready = [sem(f"row_ready{n}") for n in range(2)]
        x_added = [sem(f"x_added{n}") for n in range(2)]
        row_out = [sem(f"row_stored{n}") for n in range(2)]
        zeros = sem("zeros_ready")
        deg_done = sem("deg_done")
        deg_ready = sem("deg_clamped")
        root_ready = sem("deg_root_ready")
        link2 = sem("stage2_chain")
        passed = sem("stage2_sp_passed")
        STEP = 2
        N_STEPS = z.NT // STEP
        UNROLL = 7

        def over_steps(step, eng):
            for i in range(UNROLL):
                step(i, i, False)
            with eng.Fori(1, N_STEPS // UNROLL - 1) as j:
                for i in range(UNROLL):
                    step(j * UNROLL + i, i, False)
            for i in range(UNROLL):
                step(N_STEPS - UNROLL + i, i, True)

        with nc.Block() as block:
            @block.gpsimd
            def _(pool):
                with pool.Fori(0, N_STEPS) as i:
                    for s in range(STEP):
                        pool.wait_ge(row_ready[s], i + 1)
                        row = base_row[:, s:s + 1, :]
                        nc.gpsimd.tensor_tensor(row, row, t["x_all"][:, ds(i * STEP + s, 1), :], ALU.add).then_inc(x_added[s], 1)

            @block.sync
            def _(sp):
                def step(i):
                    for s in range(STEP):
                        sp.wait_ge(x_added[s], i + 1)
                        hold(sp, passed)
                        sp.dma_start(dram["base_out"][ds((i * STEP + s) * P, P), :], base_row[:, s, :]).then_inc(row_out[s], 16)

                with sp.Fori(0, N_STEPS) as i:
                    step(i)
                for s in range(STEP):
                    sp.wait_ge(row_out[s], 16 * N_STEPS)
                sp.wait_ge(stored, 96)

            @block.scalar
            def _(act):
                act.wait_ge(var_ready, 1)
                nc.scalar.activation(std[:, :], var[:, :], ACT.Sqrt, bias=t["eps"][:, :]).then_inc(std_ready, 1)
                act.wait_ge(norm_ready, 2)

                def layernorm(i):
                    for s in range(STEP):
                        tile = i * STEP + s
                        at_least(act, turned[s], i)
                        nc.scalar.activation(h[:, s, :].rearrange("p (a d) -> p a d", a=1), t["x_all"][:, ds(tile, 1), :],
                                             ACT.Relu, bias=t["shift"][:, ds(tile, 1)],
                                             scale=t["rstd"][:, ds(tile, 1)]).then_inc(h_ready[s], 1)

                def step(i, in_body, last):
                    for s in range(STEP):
                        act.wait_ge(turned[s], i + 1)
                        at_least(act, summed[s], i)
                        nc.scalar.copy(h_t[:, s, :], ps_turn[s][:, 0:D]).then_inc(t_ready[s], 1)
                    if not (last and in_body == UNROLL - 1):
                        layernorm(i + 1)
                    for s in range(STEP):
                        act.wait_ge(summed[s], i + 1)
                        at_least(act, row_out[s], 16 * i)
                        nc.scalar.copy(base_row[:, s, :], ps_out[s][:, 0:D]).then_inc(row_ready[s], 1)

                layernorm(0)
                over_steps(step, act)
                act.wait_ge(deg_ready, 1)
                nc.scalar.activation(deg[:, :], deg[:, :], ACT.Sqrt).then_inc(root_ready, 1)

            @block.tensor
            def _(pe):
                pe.wait_ge(zeros, 1)
                nc.tensor.matmul(ps_deg[:, 0:HI], zero_b[:, :], zero_b[:, 0:HI], start=True, stop=False)

                def count(n, b):
                    pe.wait_ge(onehots, n + 1)
                    for k in range(SLOT):
                        mm = nc.tensor.matmul(ps_deg[:, 0:HI], one_lo[:, b, :, k], one_hi[:, b, :, k],
                                              start=False, stop=False)
                    mm.then_inc(counted, 1)

                def step(i, in_body, last):
                    for s in range(STEP):
                        pe.wait_ge(h_ready[s], i + 1)
                        at_least(pe, t_ready[s], i)
                        for a in range(2):
                            mm = nc.tensor.transpose(ps_turn[s][:, a * P:a * P + P], h[:, s, a * P:a * P + P], t["ident"][:, :])
                        mm.then_inc(turned[s], 1)
                    for s in range(STEP):
                        if not last or in_body * STEP + s < STEP * UNROLL - SLOTS:
                            count(i * STEP + s + SLOTS, (in_body * STEP + s) % SLOTS)
                        pe.wait_ge(t_ready[s], i + 1)
                        at_least(pe, row_ready[s], i)
                        nc.tensor.matmul(ps_out[s][:, 0:D], t["minus_ones"][:, :], t["upd_b2"][:, :], start=True, stop=False)
                        for a in range(2):
                            mm = nc.tensor.matmul(ps_out[s][:, 0:D], h_t[:, s, a * P:a * P + P], t["upd_k"][:, a, :],
                                                  start=False, stop=(a == 1))
                        mm.then_inc(summed[s], 1)

                for b in range(SLOTS):
                    count(b, b)
                over_steps(step, pe)
                nc.tensor.matmul(ps_deg[:, 0:HI], zero_b[:, :], zero_b[:, 0:HI], start=False, stop=True).then_inc(deg_done, 1)

            @block.vector
            def _(dve):
                def build_onehots(tile, b):
                    chunks = ds(tile * SLOT, SLOT)
                    nc.vector.tensor_tensor(one_lo[:, b, :, :], t["iota_k"][:, :, :],
                                            t["src_lo"][:, chunks].rearrange("p (a k) -> p a k", a=1).to_broadcast((P, P, SLOT)),
                                            ALU.is_equal)
                    nc.vector.tensor_tensor(one_hi[:, b, :, :], t["iota_k"][:, 0:HI, :],
                                            t["src_hi"][:, chunks].rearrange("p (a k) -> p a k", a=1).to_broadcast((P, HI, SLOT)),
                                            ALU.is_equal).then_inc(onehots, 1)

                nc.vector.memset(zero_b[:, :], 0.0).then_inc(zeros, 1)
                for b in range(SLOTS):
                    build_onehots(b, b)
                dve.wait_ge(x_in, 16 * (z.NT // 14 + 1))
                with dve.Fori(0, z.NT // 14) as i:
                    for k in range(14):
                        tile = ds(i * 14 + k, 1)
                        nc.vector.bn_stats(stats[:, tile, :].rearrange("p a c -> p (a c)"),
                                           t["x_all"][:, tile, :].rearrange("p a d -> p (a d)")).then_inc(stats_ready, 1)
                dve.wait_ge(stats_ready, z.NT)
                nc.vector.tensor_tensor(mean[:, :], stats[:, :, 1], stats[:, :, 4], ALU.add).then_inc(moments, 1)
                nc.vector.tensor_tensor(half[:, :], stats[:, :, 1], stats[:, :, 4], ALU.subtract).then_inc(moments, 1)
                nc.vector.tensor_tensor(var[:, :], stats[:, :, 2], stats[:, :, 5], ALU.add).then_inc(moments, 1)
                dve.wait_ge(moments, 2)
                nc.vector.scalar_tensor_tensor(out=half[:, :], in0=half[:, :], scalar=0.25, in1=half[:, :],
                                               op0=ALU.mult, op1=ALU.mult).then_inc(moments, 1)
                dve.wait_ge(moments, 4)
                nc.vector.scalar_tensor_tensor(out=var[:, :], in0=var[:, :], scalar=1.0 / D, in1=half[:, :],
                                               op0=ALU.mult, op1=ALU.add).then_inc(var_ready, 1)
                dve.wait_ge(std_ready, 1)
                nc.vector.reciprocal(t["rstd"][:, :], std[:, :]).then_inc(norm_ready, 1)
                dve.wait_ge(norm_ready, 1)
                nc.vector.scalar_tensor_tensor(out=t["shift"][:, :], in0=mean[:, :], scalar=-0.5, in1=t["rstd"][:, :],
                                               op0=ALU.mult, op1=ALU.mult).then_inc(norm_ready, 1)

                with dve.Fori(1, z.NT // SLOTS) as i:
                    for b in range(SLOTS):
                        dve.wait_ge(counted, i * SLOTS + b + 1 - SLOTS)
                        build_onehots(i * SLOTS + b, b)
                dve.wait_ge(deg_done, 1)
                nc.vector.tensor_scalar(deg[:, :], ps_deg[:, 0:HI], 1.0, None, ALU.max).then_inc(deg_ready, 1)
                dve.wait_ge(root_ready, 1)
                nc.vector.reciprocal(t["src_norm"][:, :], deg[:, :]).then_inc(link2, 1)
                dve.wait_ge(link2, 1)
                nc.vector.tensor_tensor(t["rstd"][:, :], t["rstd"][:, :], t["src_norm"][:, :], ALU.mult).then_inc(link2, 1)
                nc.vector.tensor_tensor(t["shift"][:, :], t["shift"][:, :], t["src_norm"][:, :], ALU.mult).then_inc(link2, 1)


def stage_3(nc, z, dram, t):
    ctx = ExitStack()
    with ctx:
        def sem(name):
            return t["sems"].enter_context(nc.semaphore(name))

        LOT = 7
        BY_ACT = 5
        BUFS = 7
        rows = [ctx.enter_context(nc.sbuf_tensor(f"hs_rows{s}", [P, LOT, z.DX], F32)) for s in range(BUFS)]
        zeros = ctx.enter_context(nc.sbuf_tensor("zeros", [P, LOT, D], F32))
        act_done = sem("hs_act")
        dve_half = sem("hs_scaled")
        dve_done = sem("hs_dve")
        zeroed = sem("x_zeroed_again")
        passed = sem("stage3_sp_passed")
        out = [sem(f"hs_stored{s}") for s in range(BUFS)]
        STEPS = z.NT // (BUFS * LOT)

        with nc.Block() as block:
            @block.sync
            def _(sp):
                with sp.Fori(0, STEPS) as i:
                    for s in range(BUFS):
                        sp.wait_ge(act_done, (i * BUFS + s + 1) * BY_ACT)
                        hold(sp, passed)
                        sp.wait_ge(dve_done, (i * BUFS + s + 1) * 2)
                        hold(sp, passed)
                        sp.dma_start(dram["h_tab"][ds((i * BUFS + s) * (LOT * P), LOT * P), :].rearrange("(t p) d -> p t d", p=P),
                                     rows[s][:, :, :]).then_inc(out[s], 16)
                for s in range(BUFS):
                    sp.wait_ge(out[s], 16 * STEPS)

            @block.scalar
            def _(act):
                def step(i):
                    for s in range(BUFS):
                        at_least(act, out[s], 16 * i)
                        for k in range(BY_ACT):
                            tile = (i * BUFS + s) * LOT + k
                            nc.scalar.activation(rows[s][:, k:k + 1, 0:D], t["x_all"][:, ds(tile, 1), :],
                                                 ACT.Relu, bias=t["shift"][:, ds(tile, 1)],
                                                 scale=t["rstd"][:, ds(tile, 1)]).then_inc(act_done, 1)
                step(0)
                with act.Fori(1, STEPS) as i:
                    step(i)

            @block.vector
            def _(dve):
                def step(i):
                    for s in range(BUFS):
                        at_least(dve, out[s], 16 * i)
                        for k in range(BY_ACT, LOT):
                            tile = (i * BUFS + s) * LOT + k
                            nc.vector.tensor_scalar(rows[s][:, k:k + 1, 0:D], t["x_all"][:, ds(tile, 1), :],
                                                    t["rstd"][:, ds(tile, 1)], t["shift"][:, ds(tile, 1)],
                                                    ALU.mult, ALU.add).then_inc(dve_half, 1)
                        nc.vector.tensor_copy(rows[s][:, :, D], t["src_norm"][:, ds((i * BUFS + s) * LOT, LOT)]).then_inc(dve_done, 1)
                        dve.wait_ge(dve_half, (i * BUFS + s + 1) * (LOT - BY_ACT))
                        nc.vector.tensor_scalar(rows[s][:, BY_ACT:LOT, 0:D], rows[s][:, BY_ACT:LOT, 0:D], 0.0, None,
                                                ALU.max).then_inc(dve_done, 1)
                        dve.wait_ge(act_done, (i * BUFS + s + 1) * BY_ACT)
                        nc.vector.tensor_copy(t["x_all"][:, ds((i * BUFS + s) * LOT, LOT), :], zeros[:, :, :]).then_inc(zeroed, 1)
                nc.vector.memset(zeros[:, :, :], 0.0).then_inc(zeroed, 1)
                dve.wait_ge(zeroed, 1)
                step(0)
                with dve.Fori(1, STEPS) as i:
                    step(i)


def stage_4(nc, z, dram, t):
    ctx = ExitStack()
    with ctx:
        def sb(name, shape, dt):
            return ctx.enter_context(nc.sbuf_tensor(name, shape, dt))

        def sem(name):
            return t["sems"].enter_context(nc.semaphore(name))

        PAIRS = BODY // 2
        L = z.STEPS - 1
        hrow = sb("hrow", [P, BODY, z.DX], F32)
        high = sb("high", [P, BODY, z.DM], F32R)
        low = sb("low", [P, BODY, z.DM], F32R)
        member = sb("member", [P, BODY, WIN], F32R)
        typ_b = sb("typ_b", [P, 2, GRP * P], F16)
        one = sb("one", [P, 2, z.KT, GRP * P], F32R)
        idx = sb("idx", [P, 2, 2, GRP], I32)
        dst_g = sb("dst_g", [P, GRP], I16)
        typ_g = sb("typ_g", [P, GRP], I16)
        place_g = sb("place_g", [P, GRP], F32)
        idx_g = sb("idx_g", [P, 2 * GRP], I32)
        ps_rel = [ctx.enter_context(nc.psum_tensor(f"ps_rel{n}", [P, 2, 512], F32)) for n in range(2)]
        ps_sum = [ctx.enter_context(nc.psum_tensor(f"ps_sum{n}", [P, 512], F32)) for n in range(2)]

        consts = sem("ends_set")
        zeroed = sem("acc_zeroed")
        idx_ready = [sem(f"idx_ready{g}") for g in range(2)]
        h_in = [sem(f"hrow_in{k}") for k in range(BODY)]
        typ_in = [sem(f"typ_in{g}") for g in range(2)]
        one_ready = [sem(f"one_ready{g}") for g in range(2)]
        typ_off = [sem(f"typ_off_ready{g}") for g in range(2)]
        one_last = [sem(f"one_last_ready{g}") for g in range(2)]
        rel_ready = [sem(f"rel_ready{q}") for q in range(PAIRS)]
        msg_ready = [sem(f"msg_ready{q}") for q in range(PAIRS)]
        high_ready = [sem(f"high_ready{q}") for q in range(PAIRS)]
        distance = sem("distance_ready")
        low_ready = [sem(f"low_ready{q}") for q in range(PAIRS)]
        summed = [sem(f"summed{q}") for q in range(PAIRS)]
        added = [sem(f"added{g}") for g in range(2)]
        passed = [sem(f"passed_{n}") for n in ("pool", "sp", "dve")]
        g_in, g_set, g_rows, g_msg, g_high, g_low, g_place, g_member, g_sum, g_added = (
            sem(n) for n in ("g_in", "g_set", "g_rows", "g_msg", "g_high", "g_low", "g_place", "g_member", "g_sum",
                             "g_added"))

        def fast_or_general(eng, fast, general=None):
            outside = eng.value_load(t["flag"][0:1, 0:1], min_val=0, max_val=z.CH * P)
            with eng.If(outside == 0):
                fast()
            if general:
                with eng.Else():
                    general()

        def over_steps(eng, step):
            step(0, 0, True, False)
            with eng.Fori(0, (L - 1) // 2) as j:
                step(2 * j + 1, 1, False, False)
                step(2 * j + 2, 0, False, False)
            step(L, L % 2, False, True)

        def places(q):
            return slice(2 * q, 2 * q + 2)

        def with_step(q, i):
            return q % PAIRS, i + 1 + q // PAIRS

        with nc.Block() as block:
            @block.sync
            def _(sp):
                def load(i, g):
                    at_least(sp, one_ready[g], i)
                    hold(sp, passed[1])
                    at_least(sp, one_last[g], i)
                    hold(sp, passed[1])
                    sp.dma_start(typ_b[:, g, :], dram["typ_row"][ds(i * (BODY * P) + g * GRP * P, GRP * P)].rearrange(
                        "(a n) -> a n", a=1).to_broadcast((P, GRP * P))).then_inc(typ_in[g], 16)

                def fast():
                    load(0, 0)
                    load(0, 1)
                    with sp.Fori(1, z.STEPS) as i:
                        load(i, 0)
                        load(i, 1)

                def general():
                    def group(g):
                        at_least(sp, g_set, g)
                        hold(sp, passed[1])
                        sp.dma_start(dst_g[:, :], dram["dst_cols"][:, ds(g * GRP, GRP)]).then_inc(g_in, 16)
                        sp.dma_start(typ_g[:, :], dram["typ_cols"][:, ds(g * GRP, GRP)]).then_inc(g_in, 16)
                    group(0)
                    with sp.Fori(1, z.NG) as g:
                        group(g)

                fast_or_general(sp, fast, general)

            @block.gpsimd
            def _(pool):
                def gather(rows, table, index, landed):
                    nc.gpsimd.indirect_dma_start(rows, None, dram[table], bass.IndirectOffsetOnAxis(ap=index, axis=0)
                                                 ).then_inc(landed, 16)

                def fast():
                    def step(i, odd, first, last):
                        for k in range(BODY):
                            if k % GRP == 0:
                                pool.wait_ge(idx_ready[k // GRP], i + 1)
                            if k % 2 == 0:
                                at_least(pool, low_ready[k // 2], i)
                                hold(pool, passed[0])
                            gather(hrow[:, k, :], "h_tab", idx[:, odd, k // GRP, k % GRP:k % GRP + 1], h_in[k])
                    over_steps(pool, step)

                def general():
                    with pool.Fori(0, z.NG) as g:
                        pool.wait_ge(g_set, g + 1)
                        hold(pool, passed[0])
                        for k in range(GRP):
                            gather(hrow[:, k, :], "h_tab", idx_g[:, k:k + 1], g_rows)
                            gather(hrow[:, GRP + k, :], "rg_tab", idx_g[:, GRP + k:GRP + k + 1], g_rows)

                fast_or_general(pool, fast, general)

            @block.scalar
            def _(act):
                def fast():
                    def indices(i, odd, g):
                        for k in range(g * GRP, (g + 1) * GRP):
                            at_least(act, h_in[k], 16 * (i - 1))
                        nc.scalar.copy(idx[:, odd, g, :], t["src16"][:, ds(i * BODY + g * GRP, GRP)]).then_inc(idx_ready[g], 1)

                    def members(i, q):
                        at_least(act, summed[q], i)
                        for c in (2 * q, 2 * q + 1):
                            nc.scalar.activation(member[:, c, :], t["iota"][:, :], ACT.Abs,
                                                 bias=t["minus_place"][:, ds(i * BODY + c, 1)]).then_inc(distance, 1)
                        pair = member[:, 2 * q:2 * q + 2, :]
                        act.wait_ge(distance, (i * PAIRS + q) * 2 + 2)
                        nc.scalar.activation(pair, pair.bitcast(F32), ACT.Relu, bias=1.0, scale=-1.0)

                    def split(i, q):
                        at_least(act, summed[q], i)
                        act.wait_ge(msg_ready[q], i + 1)
                        nc.scalar.copy(high[:, places(q), 0:z.DX], hrow[:, 2 * q:2 * q + 2, :]).then_inc(high_ready[q], 1)

                    def last_distances(i, g):
                        act.wait_ge(typ_in[g], 16 * i + 16)
                        at_least(act, rel_ready[2 * g + 1], i)
                        nc.scalar.activation(one[:, g, z.KT - 1, :], typ_b[:, g, :], ACT.Abs,
                                             bias=t["rel_id"][:, z.KT - 1:z.KT], scale=-1.0).then_inc(typ_off[g], 1)

                    def last_onehots(i, g):
                        act.wait_ge(typ_off[g], i + 1)
                        nc.scalar.activation(one[:, g, z.KT - 1, :], one[:, g, z.KT - 1, :].bitcast(F32), ACT.Relu,
                                             bias=1.0, scale=-1.0).then_inc(one_last[g], 1)

                    def step(i, odd, first, last):
                        if not last:
                            indices(i + 1, 1 - odd, 0)
                            indices(i + 1, 1 - odd, 1)
                        split(i, 0)
                        last_onehots(i, 1)
                        members(i, 1)
                        split(i, 1)
                        members(i, 2)
                        if not last:
                            last_distances(i + 1, 0)
                        split(i, 2)
                        if not last:
                            last_onehots(i + 1, 0)
                        members(i, 3)
                        split(i, 3)
                        if not last:
                            members(i + 1, 0)
                            last_distances(i + 1, 1)

                    indices(0, 0, 0)
                    indices(0, 0, 1)
                    last_distances(0, 0)
                    last_onehots(0, 0)
                    members(0, 0)
                    last_distances(0, 1)
                    over_steps(act, step)

                fast_or_general(act, fast)

            @block.tensor
            def _(pe):
                def fast():
                    def relate(i, q):
                        g = q // 2
                        if q % 2 == 0:
                            pe.wait_ge(one_ready[g], i + 1)
                            pe.wait_ge(one_last[g], i + 1)
                        r, n = with_step(q - 2, i)
                        at_least(pe, msg_ready[r], n)
                        for c in range(2):
                            for k in range(z.KT):
                                for a in range(2):
                                    mm = nc.tensor.matmul(
                                        ps_rel[q % 2][:, c, 0:z.DM],
                                        one[:, g, k, ((q % 2) * 2 + c) * P:((q % 2) * 2 + c + 1) * P],
                                        t["table"][:, k, a, :], start=(k == 0 and a == 0), stop=(k == z.KT - 1 and a == 1))
                        mm.then_inc(rel_ready[q], 1)

                    def add(i, q):
                        g = q // 2
                        pe.wait_ge(high_ready[q], i + 1)
                        pe.wait_ge(low_ready[q], i + 1)
                        if q % 2 == 0:
                            at_least(pe, added[g], 2 * i)
                        for c in range(2):
                            for a, half in enumerate((high, low)):
                                mm = nc.tensor.matmul(ps_sum[g][:, 0:z.DM], member[:, 2 * q + c, :], half[:, 2 * q + c, :],
                                                      start=(q % 2 == 0 and c == 0 and a == 0),
                                                      stop=(q % 2 == 1 and c == 1 and a == 1))
                        mm.then_inc(summed[q], 1)

                    def step(i, odd, first, last):
                        relate(i, 0)
                        if not first:
                            add(i - 1, 2)
                        relate(i, 1)
                        if not first:
                            add(i - 1, 3)
                        relate(i, 2)
                        add(i, 0)
                        relate(i, 3)
                        add(i, 1)

                    pe.wait_ge(consts, 2)
                    over_steps(pe, step)
                    add(L, 2)
                    add(L, 3)

                def general():
                    with pe.Fori(0, z.NG * z.NT) as u:
                        pe.wait_ge(g_member, u + 1)
                        for k in range(GRP):
                            for a, half in enumerate((high, low)):
                                mm = nc.tensor.matmul(ps_sum[0][:, 0:z.DM], member[:, k, :], half[:, k, :],
                                                      start=(k == 0 and a == 0), stop=(k == GRP - 1 and a == 1))
                        mm.then_inc(g_sum, 1)

                fast_or_general(pe, fast, general)

            @block.vector
            def _(dve):
                nc.vector.memset(high[:, :, z.DM - 1:z.DM].bitcast(F32), 1.0).then_inc(consts, 1)
                nc.vector.memset(low[:, :, z.DM - 1:z.DM].bitcast(F32), 0.0).then_inc(consts, 1)
                acc = t["acc"][:, :, :].rearrange("p t d -> p (t d)")
                nc.vector.memset(acc[:, z.NT * D:(z.NT + 1) * z.DM], 0.0).then_inc(zeroed, 1)
                dve.wait_ge(consts, 2)
                dve.wait_ge(zeroed, 1)

                def fast():
                    def onehots(i, g, tiles):
                        if tiles[0] == 0:
                            dve.wait_ge(typ_in[g], 16 * i + 16)
                            at_least(dve, rel_ready[2 * g + 1], i)
                        for k in tiles:
                            last = nc.vector.tensor_scalar(one[:, g, k, :], typ_b[:, g, :], t["rel_id"][:, k:k + 1], None,
                                                           ALU.is_equal)
                        if tiles[-1] == z.KT - 2:
                            last.then_inc(one_ready[g], 1)

                    def multiply(i, q):
                        for k in (2 * q, 2 * q + 1):
                            dve.wait_ge(h_in[k], 16 * i + 16)
                        dve.wait_ge(rel_ready[q], i + 1)
                        rows = hrow[:, 2 * q:2 * q + 2, :]
                        nc.vector.tensor_tensor(rows, ps_rel[q % 2][:, :, 0:z.DX], rows, ALU.mult).then_inc(msg_ready[q], 1)

                    def rest(i, q):
                        dve.wait_ge(high_ready[q], i + 1)
                        nc.vector.tensor_tensor(low[:, places(q), 0:z.DX], hrow[:, 2 * q:2 * q + 2, :],
                                                high[:, places(q), 0:z.DX].bitcast(F32), ALU.subtract).then_inc(low_ready[q], 1)

                    def add(i, g):
                        tile = dve.value_load(t["tile_id"][0:1, ds(2 * i + g, 1)], min_val=0, max_val=z.NT - 1)
                        dve.wait_ge(summed[2 * g + 1], i + 1)
                        if g == 0:
                            at_least(dve, added[1], 2 * i)
                        else:
                            dve.wait_ge(added[0], 2 * i + 2)
                        for n in range(2):
                            nodes = t["acc"][:, ds(tile + n, 1), :].rearrange("p a d -> p (a d)")
                            nc.vector.scalar_tensor_tensor(out=nodes, in0=ps_sum[g][:, 0:z.DM],
                                                           scalar=t["mask"][:, n, ds(2 * i + g, 1)], in1=nodes,
                                                           op0=ALU.mult, op1=ALU.add).then_inc(added[g], 1)

                    begun, others = list(range(z.KT - 2)), [z.KT - 2]

                    def step(i, odd, first, last):
                        multiply(i, 0)
                        onehots(i, 1, others)
                        if not first:
                            rest(i - 1, 3)
                            add(i - 1, 0)
                        multiply(i, 1)
                        rest(i, 0)
                        if not last:
                            onehots(i + 1, 0, begun)
                        multiply(i, 2)
                        if not last:
                            onehots(i + 1, 0, others)
                        rest(i, 1)
                        if not first:
                            add(i - 1, 1)
                        multiply(i, 3)
                        rest(i, 2)
                        if not last:
                            onehots(i + 1, 1, begun)

                    onehots(0, 0, begun + others)
                    onehots(0, 1, begun)
                    over_steps(dve, step)
                    rest(L, 3)
                    add(L, 0)
                    add(L, 1)

                def general():
                    def group(g):
                        dve.wait_ge(g_in, 32 * g + 32)
                        nc.vector.tensor_copy(place_g[:, :], dst_g[:, :]).then_inc(g_place, 1)
                        nc.vector.tensor_copy(idx_g[:, 0:GRP], t["src16"][:, ds(g * GRP, GRP)])
                        nc.vector.tensor_copy(idx_g[:, GRP:2 * GRP], typ_g[:, :]).then_inc(g_set, 1)
                        dve.wait_ge(g_rows, (g + 1) * (2 * GRP * 16))
                        rows = hrow[:, 0:GRP, :]
                        nc.vector.tensor_tensor(rows, rows, hrow[:, GRP:2 * GRP, :], ALU.mult).then_inc(g_msg, 1)
                        dve.wait_ge(g_msg, g + 1)
                        hold(dve, passed[2])
                        nc.vector.tensor_copy(high[:, 0:GRP, 0:z.DX], rows).then_inc(g_high, 1)
                        dve.wait_ge(g_high, g + 1)
                        nc.vector.tensor_tensor(low[:, 0:GRP, 0:z.DX], rows, high[:, 0:GRP, 0:z.DX].bitcast(F32),
                                                ALU.subtract).then_inc(g_low, 1)
                        dve.wait_ge(g_low, g + 1)
                        hold(dve, passed[2])
                        with dve.Fori(0, z.NT) as w:
                            u = g * z.NT + w
                            dve.wait_ge(g_place, g * (z.NT + 1) + w + 1)
                            for k in range(GRP):
                                last = nc.vector.tensor_scalar(member[:, k, :], t["iota"][:, :], place_g[:, k:k + 1], None,
                                                               ALU.is_equal)
                            last.then_inc(g_member, 1)
                            dve.wait_ge(g_member, u + 1)
                            nc.vector.tensor_scalar(place_g[:, :], place_g[:, :], -float(WIN), None,
                                                    ALU.add).then_inc(g_place, 1)
                            dve.wait_ge(g_sum, u + 1)
                            nodes = t["acc"][:, ds(w, 1), :].rearrange("p a d -> p (a d)")
                            nc.vector.tensor_tensor(nodes, ps_sum[0][:, 0:z.DM], nodes, ALU.add).then_inc(g_added, 1)
                            dve.wait_ge(g_added, u + 1)
                            hold(dve, passed[2])

                    with dve.Fori(0, z.NG) as g:
                        group(g)

                fast_or_general(dve, fast, general)


def stage_5(nc, z, dram, t, out):
    ctx = ExitStack()
    with ctx:
        def sb(name, shape, dt):
            return ctx.enter_context(nc.sbuf_tensor(name, shape, dt))

        def sem(name):
            return t["sems"].enter_context(nc.semaphore(name))

        TILES = 14
        TURN_BUFS = 7
        LOTS = [(0, 4), (4, 7), (7, 11), (11, TILES)]
        AHEAD = 2
        L = z.NT // TILES - 1
        norm = sb("in_norm", [P, z.NT], F32)
        b_norm = sb("b_norm", [P, z.NT], F32)
        one_row = sb("one_row", [1, P], F32)
        w_ext = sb("w_ext_rows", [P, D], F32)
        a_row = sb("a_row", [P, TURN_BUFS, D], F32)
        a_tile = sb("a_tile", [P, TURN_BUFS, D], F32)
        w_agg = sb("w_agg_back", [P, 2, D], F32)
        row = sb("row", [P, TILES, D], F32)
        done_row = sb("done_row", [P, TILES, D], F32)
        ps_turn = [ctx.enter_context(nc.psum_tensor(f"ps_a_turn{n}", [P, 512], F32))[:, 0:D] for n in range(2)]
        ps = [ctx.enter_context(nc.psum_tensor(f"ps_final{n}", [P, 512], F32))[:, 0:D] for n in range(2)]
        ps_w = ctx.enter_context(nc.psum_tensor("ps_w_ext", [P, 512], F32))
        w_in = sem("w_agg_loaded")
        ones_set = sem("one_row_set")
        w_ext_ps = sem("w_ext_in_psum")
        deg_ready = sem("in_deg_clamped")
        root_ready = sem("in_deg_root")
        norm_ready = sem("in_norm_ready")
        row_in = [sem(f"row_in{n}") for n in range(len(LOTS))]
        staged = sem("a_staged")
        turned = sem("a_turned")
        tile_ready = sem("tile_ready")
        product = sem("product")
        b_added = sem("b_added")
        row_done = sem("row_done")
        row_out = [sem(f"final_stored{n}") for n in range(len(LOTS))]
        passed = [sem(f"stage5_{n}_passed") for n in ("sp", "pool")]

        def over_tiles(eng, do, ahead=None, by=0):
            def body(i, last):
                for s in range(TILES):
                    if ahead and (s + by < TILES or not last):
                        ahead(i * TILES + s + by, (s + by) % TILES)
                    do(i * TILES + s, s, i)
            for s in range(by):
                ahead(s, s)
            body(0, False)
            with eng.Fori(1, L) as i:
                body(i, False)
            body(L, True)

        with nc.Block() as block:
            @block.sync
            def _(sp):
                sp.dma_start(w_agg[:, :, :], dram["w_agg"].rearrange("h p d -> p h d")).then_inc(w_in, 16)

                def step(i):
                    for n, (s0, s1) in enumerate(LOTS):
                        at_least(sp, row_done, (i - 1) * TILES + s1)
                        hold(sp, passed[0])
                        sp.dma_start(row[:, s0:s1, :], dram["base_out"][ds(i * (TILES * P) + s0 * P, (s1 - s0) * P), :].rearrange(
                            "(t p) d -> p t d", p=P)).then_inc(row_in[n], 16)
                step(0)
                with sp.Fori(1, L + 1) as i:
                    step(i)

            @block.gpsimd
            def _(pool):
                def store(i, n, s0, s1):
                    pool.wait_ge(row_done, i * TILES + s1)
                    hold(pool, passed[1])
                    pool.dma_start(out[ds(i * (TILES * P) + s0 * P, (s1 - s0) * P), :].rearrange("(t p) d -> p t d", p=P),
                                   done_row[:, s0:s1, :]).then_inc(row_out[n], 16)

                with pool.Fori(0, L) as i:
                    for n, (s0, s1) in enumerate(LOTS):
                        store(i, n, s0, s1)
                for n, (s0, s1) in enumerate(LOTS):
                    store(L, n, s0, min(s1, TILES - 1))
                pool.wait_ge(row_done, z.NT)
                pool.dma_start(out[(z.NT - 1) * P:z.N, :], done_row[0:z.LAST, TILES - 1, :]).then_inc(row_out[-1], 16)
                for n in range(len(LOTS) - 1):
                    pool.wait_ge(row_out[n], 16 * (L + 1))
                pool.wait_ge(row_out[-1], 16 * (L + 2))

            @block.scalar
            def _(act):
                act.wait_ge(deg_ready, 1)
                nc.scalar.activation(norm[:, :], norm[:, :], ACT.Sqrt).then_inc(root_ready, 1)

                def stage(tile, s):
                    at_least(act, turned, tile - TURN_BUFS + 1)
                    nc.scalar.copy(a_row[:, s % TURN_BUFS:s % TURN_BUFS + 1, :], t["acc"][:, ds(tile, 1), 0:D]).then_inc(staged, 1)

                def unload(tile, s, i):
                    act.wait_ge(turned, tile + 1)
                    at_least(act, product, tile - TURN_BUFS + 1)
                    nc.scalar.copy(a_tile[:, s % TURN_BUFS, :], ps_turn[s % 2]).then_inc(tile_ready, 1)
                over_tiles(act, unload, stage, AHEAD + 1)

            @block.tensor
            def _(pe):
                def turn(tile, s):
                    pe.wait_ge(staged, tile + 1)
                    at_least(pe, tile_ready, tile - 1)
                    for a in range(2):
                        mm = nc.tensor.transpose(ps_turn[s % 2][:, a * P:a * P + P], a_row[:, s % TURN_BUFS, a * P:a * P + P],
                                                 t["ident"][:, :])
                    mm.then_inc(turned, 1)

                def multiply(tile, s, i):
                    pe.wait_ge(tile_ready, tile + 1)
                    at_least(pe, row_done, tile - 1)
                    for a in range(2):
                        mm = nc.tensor.matmul(ps[s % 2], a_tile[:, s % TURN_BUFS, a * P:a * P + P], w_agg[:, a, :],
                                              start=(a == 0), stop=(a == 1))
                    mm.then_inc(product, 1)

                pe.wait_ge(ones_set, 1)
                nc.tensor.matmul(ps_w[:, 0:D], one_row[:, :], t["w_ext"][:, :], start=True, stop=True).then_inc(w_ext_ps, 1)
                pe.wait_ge(w_in, 16)
                over_tiles(pe, multiply, turn, AHEAD)

            @block.vector
            def _(dve):
                nc.vector.memset(one_row[:, :], 1.0).then_inc(ones_set, 1)
                nc.vector.tensor_scalar(norm[:, :], t["acc"][:, 0:z.NT, D + 1], 1.0, None, ALU.max).then_inc(deg_ready, 1)
                dve.wait_ge(w_ext_ps, 1)
                nc.vector.tensor_copy(w_ext[:, :], ps_w[:, 0:D]).then_inc(norm_ready, 1)
                dve.wait_ge(root_ready, 1)
                nc.vector.reciprocal(norm[:, :], norm[:, :]).then_inc(norm_ready, 1)
                dve.wait_ge(norm_ready, 2)
                nc.vector.tensor_tensor(b_norm[:, :], t["acc"][:, 0:z.NT, D], norm[:, :], ALU.mult).then_inc(norm_ready, 1)
                dve.wait_ge(norm_ready, 3)

                def finish(tile, s, i):
                    for n, (s0, s1) in enumerate(LOTS):
                        if s == s0:
                            dve.wait_ge(row_in[n], 16 * i + 16)
                            at_least(dve, row_out[n], 16 * i)
                    nc.vector.scalar_tensor_tensor(out=row[:, s, :], in0=w_ext[:, :], scalar=b_norm[:, ds(tile, 1)],
                                                   in1=row[:, s, :], op0=ALU.mult, op1=ALU.add).then_inc(b_added, 1)
                    dve.wait_ge(product, tile + 1)
                    dve.wait_ge(b_added, tile + 1)
                    nc.vector.scalar_tensor_tensor(out=done_row[:, s, :], in0=ps[s % 2], scalar=norm[:, ds(tile, 1)],
                                                   in1=row[:, s, :], op0=ALU.mult, op1=ALU.add).then_inc(row_done, 1)
                over_tiles(dve, finish)


def gnn_layer(nc, io, out):
    z = Sizes(io["x"].shape[0], io["src"].shape[0], io["rel"].shape[0])
    dram = {
        "h_tab": nc.dram_tensor("h_tab", [z.NP, z.DX], F32).ap(),
        "rg_tab": nc.dram_tensor("rg_tab", [z.R, z.DX], F32).ap(),
        "base_out": nc.dram_tensor("base_out", [z.NP, D], F32).ap(),
        "typ_row": nc.dram_tensor("typ_row", [z.NB * P * P], F16).ap(),
        "typ_cols": nc.dram_tensor("typ_cols", [P, z.CH], I16).ap(),
        "dst_cols": nc.dram_tensor("dst_cols", [P, z.CH], I16).ap(),
        "w_agg": nc.dram_tensor("w_agg_kept", [2, P, D], F32).ap(),
    }
    with ExitStack() as keep:
        t = {"sems": keep}

        def sb(ctx, name, shape, dt):
            t[name] = ctx.enter_context(nc.sbuf_tensor(name, shape, dt))

        sb(keep, "acc", [P, z.NT + 1, z.DM], F32)
        t["x_all"] = t["acc"][:, :, :].rearrange("p t d -> p (t d)")[:, 0:z.NT * D].rearrange("p (t d) -> p t d", d=D)
        sb(keep, "ident", [P, P], F32)
        sb(keep, "iota", [P, P], F32)
        sb(keep, "eps", [P, 1], F32)
        sb(keep, "rel_id", [P, z.KT], F32)
        sb(keep, "src16", [P, z.CH], I16)
        sb(keep, "minus_place", [P, z.CH], F16)
        sb(keep, "table", [P, z.KT, 2, z.DM], F32R)
        sb(keep, "w_ext", [1, D], F32)
        sb(keep, "tile_id", [1, z.NG], I32)
        sb(keep, "mask", [P, 2, z.NG], F32)
        sb(keep, "flag", [1, 1], I32)
        x_in = keep.enter_context(nc.semaphore("x_in"))
        with ExitStack() as early:
            sb(early, "iota_k", [P, P, COUNT], BF16)
            sb(early, "src_lo", [P, z.CH], BF16)
            sb(early, "src_hi", [P, z.CH], BF16)
            sb(early, "upd_k", [P, 2, D], F32)
            sb(early, "upd_b2", [2, D], F32R)
            sb(early, "minus_ones", [2, P], F32R)
            sb(early, "rstd", [P, z.NT], F32)
            sb(early, "shift", [P, z.NT], F32)
            sb(early, "src_norm", [P, z.NT], F32)
            sb(early, "rows_h", [P, z.NB, P], F16)
            sb(early, "dst16", [P, z.CH], I16)
            sb(early, "typ16", [P, z.CH], I16)
            sb(early, "gated", [P, z.KT, z.DM], F32)
            sb(early, "w_agg", [P, 2, D], F32)
            stored = keep.enter_context(nc.semaphore("lists_stored"))
            stage_1(nc, z, io, dram, t, x_in, stored)
            stage_2(nc, z, dram, t, x_in, stored)
            stage_3(nc, z, dram, t)
        stage_4(nc, z, dram, t)
        stage_5(nc, z, dram, t, out)


def kernel(x, src, dst, edge_type_500, L0_gnn_relation_emb, L0_gnn_msg_w, L0_gnn_msg_b, L0_gnn_upd_w, L0_gnn_upd_b,
           L0_gnn_gate_w, L0_gnn_gate_b):
    import numpy as np
    import concourse.bacc as bacc
    from concourse.bass_utils import run_bass_kernel_spmd

    laid_out = {
        "x": np.asarray(x),
        "src": np.asarray(src),
        "dst": np.asarray(dst),
        "typ": np.asarray(edge_type_500),
        "rel": np.asarray(L0_gnn_relation_emb),
        "msg_w": np.asarray(L0_gnn_msg_w).transpose(1, 0, 2),
        "msg_b": np.asarray(L0_gnn_msg_b).reshape(2, P).T,
        "upd_w": np.asarray(L0_gnn_upd_w).transpose(2, 1, 0),
        "upd_b": np.asarray(L0_gnn_upd_b).T.reshape(1, D),
        "gate_w": np.asarray(L0_gnn_gate_w).reshape(C, BL).T.reshape(1, D),
        "gate_b": np.asarray(L0_gnn_gate_b).reshape(1, 1),
    }
    nc = bacc.Bacc("TRN2", target_bir_lowering=False, num_devices=1)
    arrays, io = {}, {}
    for name, a in laid_out.items():
        arrays[f"in_{name}"] = np.ascontiguousarray(a)
        io[name] = nc.dram_tensor(f"in_{name}", a.shape, mybir.dt.from_np(a.dtype), kind="ExternalInput").ap()
    out = nc.dram_tensor("out", laid_out["x"].shape, F32, kind="ExternalOutput").ap()
    gnn_layer(nc, io, out)
    result = run_bass_kernel_spmd(nc, [arrays], core_ids=[0])
    return result.results[0]["out"]
```
